# Optimizing a Trainium2 kernel written in Bass

```python
import numpy as np
import jax
import jax.numpy as jnp

def _softmax(x, axis=-1):
    return jax.nn.softmax(x, axis=axis)

def _gelu(x):
    return jax.nn.gelu(x, approximate=True)

def _silu(x):
    return jax.nn.silu(x)

def _sigmoid(x):
    return jax.nn.sigmoid(x)

def _layernorm(x, axis=-1, eps=1e-05):
    m = jnp.mean(x, axis=axis, keepdims=True)
    v = jnp.var(x, axis=axis, keepdims=True)
    return (x - m) / jnp.sqrt(v + eps)

def _scatter_add(tgt, idx, src, axis=0):
    return tgt.at[idx].add(src)

def _segment_sum(src, seg, n):
    return jax.ops.segment_sum(src, seg, n)
kernel_name = 'mk_xattn_seq_d1_seqx_r4_c0c116'

def setup_inputs(seed: int=0):
    np.random.seed(seed)
    _w = jnp.asarray

    def _rec_inputs():
        import jax
        import jax.numpy as jnp
        _rk = jax.random.key(seed)
        x = -0.000296 + 1 * jax.random.normal(jax.random.fold_in(_rk, 1), (64, 256, 320), jnp.float32)
        _lenS = 256 - jax.random.randint(jax.random.fold_in(_rk, 7), (64,), 0, max(1, 256 // 4) + 1, jnp.int32)
        _lenS2 = 77 - jax.random.randint(jax.random.fold_in(_rk, 8), (64,), 0, max(1, 77 // 4) + 1, jnp.int32)
        _ctx_2048P = jax.random.normal(jax.random.fold_in(_rk, 11), (64, 16, 512), jnp.float32)
        _ctx_2048c = jax.random.dirichlet(jax.random.fold_in(_rk, 511), 0.3 * jnp.ones((16,), jnp.float32), (64, 77))
        _ctx_2048t = jnp.einsum('bsk,bkd->bsd', _ctx_2048c, _ctx_2048P)
        _ctx_2048t = _ctx_2048t * jax.lax.rsqrt(jnp.mean(jnp.square(_ctx_2048t)) + 1e-12) * 0.953939
        ctx_2048 = 0.00118529 + 0.99962 * (_ctx_2048t + 0.3 * jax.random.normal(jax.random.fold_in(_rk, 611), (64, 77, 512), jnp.float32))
        fside_Bx4x4_0 = jax.random.uniform(jax.random.fold_in(_rk, 12), (64, 4, 4), jnp.float32, 0.0, 0.981965)
        return (x, ctx_2048, fside_Bx4x4_0)
    x, ctx_2048, fside_Bx4x4_0 = _rec_inputs()

    def _L0_xattn_setup():
        import jax, jax.numpy as jnp
        import numpy as np
        HEADS = 20
        NUM_IP_TOKENS = 4
        NUM_DUMMY_TOKENS = 4
        IP_SCALE = 1.0
        ASPECT_RATIO = 1.0
        NEG = -10000.0

        def _grid_hw(seq_len, aspect_ratio):
            width = int((seq_len / aspect_ratio) ** 0.5)
            height = seq_len // width
            while width * height != seq_len:
                if width * height < seq_len:
                    width += 1
                else:
                    width -= 1
                height = seq_len // width
            return (height, width)

        def _sdpa(q, k, v, mask=None):
            dh = q.shape[-1]
            scores = jnp.einsum('bhqd,bhkd->bhqk', q, k) / jnp.sqrt(jnp.asarray(dh, q.dtype))
            if mask is not None:
                scores = scores + mask
            probs = jax.nn.softmax(scores, axis=-1)
            return jnp.einsum('bhqk,bhkd->bhqd', probs, v)

        def _split_heads(x, heads):
            b, l, d = x.shape
            return x.reshape(b, l, heads, d // heads).transpose(0, 2, 1, 3)

        def _merge_heads(x):
            b, h, l, dh = x.shape
            return x.transpose(0, 2, 1, 3).reshape(b, l, h * dh)

        def _ip_mask(bbox, batch_size, seq_len, dtype):
            M = bbox.shape[1]
            height, width = _grid_hw(seq_len, ASPECT_RATIO)
            x = jnp.linspace(0.0, 1.0, width, dtype=dtype)
            y = jnp.linspace(0.0, 1.0, height, dtype=dtype)
            yg, xg = jnp.meshgrid(y, x, indexing='ij')
            xg = xg.reshape(-1)
            yg = yg.reshape(-1)
            x1, y1, x2, y2 = (bbox[..., 0:1], bbox[..., 1:2], bbox[..., 2:3], bbox[..., 3:4])
            inside = (xg >= x1) & (xg <= x2) & (yg >= y1) & (yg <= y2)
            ip_mask = jnp.where(inside, 0.0, NEG).astype(dtype)
            ip_mask = jnp.transpose(ip_mask, (0, 2, 1))[:, None]
            ip_mask = jnp.repeat(ip_mask, NUM_IP_TOKENS // M, axis=-1)
            dummy = jnp.where(jnp.any(inside, axis=1), NEG, 0.0).astype(dtype)
            dummy = jnp.repeat(dummy[:, None, :, None], NUM_DUMMY_TOKENS, axis=-1)
            return jnp.concatenate([dummy, ip_mask], axis=-1)
        key = jax.random.key(seed)
        ks = jax.random.split(key, 12)
        B, S, D, C = (4, 1024, 320, 512)
        text_len, M = (77, 4)
        hidden_states = jax.random.normal(ks[0], (B, S, D), jnp.float32)
        encoder_hidden_states = jax.random.normal(ks[1], (B, text_len + NUM_IP_TOKENS + NUM_DUMMY_TOKENS, C), jnp.float32)
        p1 = jax.random.uniform(ks[2], (B, M, 2), jnp.float32)
        p2 = jax.random.uniform(ks[3], (B, M, 2), jnp.float32)
        bbox = jnp.concatenate([jnp.minimum(p1, p2), jnp.maximum(p1, p2)], axis=-1)
        s = 0.02
        w_q = jax.random.normal(ks[4], (D, D), jnp.float32) * s
        w_k = jax.random.normal(ks[5], (C, D), jnp.float32) * s
        w_v = jax.random.normal(ks[6], (C, D), jnp.float32) * s
        w_k_ip = jax.random.normal(ks[7], (C, D), jnp.float32) * s
        w_v_ip = jax.random.normal(ks[8], (C, D), jnp.float32) * s
        w_out = jax.random.normal(ks[9], (D, D), jnp.float32) * s
        b_out = jnp.zeros((D,), jnp.float32)
        return {'hidden_states': hidden_states, 'encoder_hidden_states': encoder_hidden_states, 'bbox': bbox, 'w_q': w_q, 'w_k': w_k, 'w_v': w_v, 'w_k_ip': w_k_ip, 'w_v_ip': w_v_ip, 'w_out': w_out, 'b_out': b_out}
    _L0_xattn_all = _L0_xattn_setup()
    _L0_xattn_in = {k: v for k, v in _L0_xattn_all.items() if k in ('w_q', 'w_k', 'w_v', 'w_k_ip', 'w_v_ip', 'w_out', 'b_out')}
    del _L0_xattn_all
    return {'x': x, 'ctx_2048': ctx_2048, 'fside_Bx4x4_0': fside_Bx4x4_0, 'L0_xattn_w_q': _L0_xattn_in['w_q'], 'L0_xattn_w_k': _L0_xattn_in['w_k'], 'L0_xattn_w_v': _L0_xattn_in['w_v'], 'L0_xattn_w_k_ip': _L0_xattn_in['w_k_ip'], 'L0_xattn_w_v_ip': _L0_xattn_in['w_v_ip'], 'L0_xattn_w_out': _L0_xattn_in['w_out'], 'L0_xattn_b_out': _L0_xattn_in['b_out']}

def reference(x, ctx_2048, fside_Bx4x4_0, L0_xattn_w_q, L0_xattn_w_k, L0_xattn_w_v, L0_xattn_w_k_ip, L0_xattn_w_v_ip, L0_xattn_w_out, L0_xattn_b_out):
    import jax
    import jax.numpy as jnp

    def _L0_xattn_ref(hidden_states, encoder_hidden_states, bbox, w_q, w_k, w_v, w_k_ip, w_v_ip, w_out, b_out):
        import jax, jax.numpy as jnp
        import numpy as np
        HEADS = 20
        NUM_IP_TOKENS = 4
        NUM_DUMMY_TOKENS = 4
        IP_SCALE = 1.0
        ASPECT_RATIO = 1.0
        NEG = -10000.0

        def _grid_hw(seq_len, aspect_ratio):
            width = int((seq_len / aspect_ratio) ** 0.5)
            height = seq_len // width
            while width * height != seq_len:
                if width * height < seq_len:
                    width += 1
                else:
                    width -= 1
                height = seq_len // width
            return (height, width)

        def _sdpa(q, k, v, mask=None):
            dh = q.shape[-1]
            scores = jnp.einsum('bhqd,bhkd->bhqk', q, k) / jnp.sqrt(jnp.asarray(dh, q.dtype))
            if mask is not None:
                scores = scores + mask
            probs = jax.nn.softmax(scores, axis=-1)
            return jnp.einsum('bhqk,bhkd->bhqd', probs, v)

        def _split_heads(x, heads):
            b, l, d = x.shape
            return x.reshape(b, l, heads, d // heads).transpose(0, 2, 1, 3)

        def _merge_heads(x):
            b, h, l, dh = x.shape
            return x.transpose(0, 2, 1, 3).reshape(b, l, h * dh)

        def _ip_mask(bbox, batch_size, seq_len, dtype):
            M = bbox.shape[1]
            height, width = _grid_hw(seq_len, ASPECT_RATIO)
            x = jnp.linspace(0.0, 1.0, width, dtype=dtype)
            y = jnp.linspace(0.0, 1.0, height, dtype=dtype)
            yg, xg = jnp.meshgrid(y, x, indexing='ij')
            xg = xg.reshape(-1)
            yg = yg.reshape(-1)
            x1, y1, x2, y2 = (bbox[..., 0:1], bbox[..., 1:2], bbox[..., 2:3], bbox[..., 3:4])
            inside = (xg >= x1) & (xg <= x2) & (yg >= y1) & (yg <= y2)
            ip_mask = jnp.where(inside, 0.0, NEG).astype(dtype)
            ip_mask = jnp.transpose(ip_mask, (0, 2, 1))[:, None]
            ip_mask = jnp.repeat(ip_mask, NUM_IP_TOKENS // M, axis=-1)
            dummy = jnp.where(jnp.any(inside, axis=1), NEG, 0.0).astype(dtype)
            dummy = jnp.repeat(dummy[:, None, :, None], NUM_DUMMY_TOKENS, axis=-1)
            return jnp.concatenate([dummy, ip_mask], axis=-1)
        B, S, D = hidden_states.shape
        residual = hidden_states
        end_pos = encoder_hidden_states.shape[1] - (NUM_IP_TOKENS + NUM_DUMMY_TOKENS)
        text = encoder_hidden_states[:, :end_pos]
        ip_h = encoder_hidden_states[:, end_pos:]
        q = _split_heads(hidden_states @ w_q, HEADS)
        k = _split_heads(text @ w_k, HEADS)
        v = _split_heads(text @ w_v, HEADS)
        out_text = _sdpa(q, k, v)
        out_text = _merge_heads(out_text)
        mask_ip = _ip_mask(bbox, B, S, hidden_states.dtype)
        k_ip = _split_heads(ip_h @ w_k_ip, HEADS)
        v_ip = _split_heads(ip_h @ w_v_ip, HEADS)
        out_ip = _merge_heads(_sdpa(q, k_ip, v_ip, mask=mask_ip))
        out = out_text + IP_SCALE * out_ip
        out = out @ w_out + b_out
        out = out + residual
        return out
    x = _L0_xattn_ref(x, ctx_2048, fside_Bx4x4_0, L0_xattn_w_q, L0_xattn_w_k, L0_xattn_w_v, L0_xattn_w_k_ip, L0_xattn_w_v_ip, L0_xattn_w_out, L0_xattn_b_out)
    return x

_drawn_inputs = setup_inputs


def setup_inputs(seed=0):
    import zlib

    import numpy as np

    out = dict(_drawn_inputs(seed))
    spreads = {'L0_xattn_b_out': (0.0, 0.1)}
    factors = {'L0_xattn_w_q': 5.553, 'L0_xattn_w_k': 8.0, 'L0_xattn_w_k_ip': 6.388}
    for name, (base, spread) in spreads.items():
        noise = np.random.default_rng([zlib.crc32(name.encode()), seed]).standard_normal(out[name].shape)
        drawn = base * np.exp(spread * noise) if base else spread * noise
        out[name] = jnp.asarray(drawn.astype(out[name].dtype))
    for name, factor in factors.items():
        out[name] = (out[name] * factor).astype(out[name].dtype)
    return out
```

```python
import numpy as np
import concourse.bass as bass
from concourse import mybir
from contextlib import ExitStack

fp32 = mybir.dt.float32
f32r = mybir.dt.float32r
bf16 = mybir.dt.bfloat16
fp16 = mybir.dt.float16
ALU = mybir.AluOpType
ACT = mybir.ActivationFunctionType
AX = mybir.AxisListType

P = 128
B, S, D, C = 64, 256, 320, 512
H, DH = 20, 16
T, NIP = 69, 8
KEYS = T + NIP
NT = S // P
GW = 16
NEG = -10000.0
SHIFT = 5.0

GROUPS = [8, 8, 4]
GHEAD = [0, 8, 16]
GTILES = [-(-g * KEYS // P) for g in GROUPS]
GTILE = [sum(GTILES[:g]) for g in range(3)]
TILES = sum(GTILES)
ROWS = TILES * P
QUAD = 4 * KEYS
QUADS = H // 4
PAIRS = -(-TILES // 2)
RING = [0, 1, 2, 0, 1, 2, 1]
UNITS = NT * 3
SLOT = 50
R_MT, R_MI, R_MASK, R_ONE = 0, H, 64, 80
KC = 4
CB = 4
CK = T + 1
DW = D + 64


def tile_parts():
    out = []
    for g, heads in enumerate(GROUPS):
        for t in range(GTILES[g]):
            r0, r1 = t * P, min((t + 1) * P, heads * KEYS)
            parts = []
            for h in range(r0 // KEYS, (r1 - 1) // KEYS + 1):
                k0, k1 = max(0, r0 - h * KEYS), min(KEYS, r1 - h * KEYS)
                for ip, (a, b) in enumerate(((k0, min(k1, T)), (max(k0, T), k1))):
                    if b > a:
                        parts.append((2 * h + ip, h * KEYS + a - r0, a, b - a))
            out.append((g, parts[0][0], parts))
    return out


PARTS = tile_parts()
NSLOTS = [p[-1][0] - s + 1 for _, s, p in PARTS]
SLOTS = max(NSLOTS)
VCOLS = TILES * SLOTS * SLOT
NVDMA = 6


def constants():
    sel = np.zeros((P, ROWS), np.float32)
    ones = np.zeros((P, VCOLS), np.float32)
    for t, (g, s0, parts) in enumerate(PARTS):
        for slot, row, key, n in parts:
            head = GHEAD[g] + slot // 2
            for r in range(n):
                col = t * P + row + r
                sel[(R_MI if slot % 2 else R_MT) + head, col] = -1.0
                if slot % 2:
                    sel[R_MASK + key + r - T, col] = 1.0
                sel[R_ONE, col] = 1.0
                c = (t * SLOTS + slot - s0) * SLOT + 1
                ones[row + r, c:c + SLOT - 1] = 1.0
    line = np.arange(GW, dtype=np.float32) * np.float32(1.0 / (GW - 1))
    grid = np.zeros((P, 4), np.float32)
    s = np.arange(P)
    grid[:, 0] = line[s % GW]
    grid[:, 1] = line[s // GW]
    grid[:, 2] = line[(s + P) // GW]
    own = np.zeros((P, 8 + 8 + 4), np.float32)
    for g, heads in enumerate(GROUPS):
        for h in range(heads):
            own[h * DH:(h + 1) * DH, GHEAD[g] + h] = 1.0
            if g == 2:
                own[64 + h * DH:64 + (h + 1) * DH, GHEAD[g] + h] = 1.0
    return {"c_sel": sel, "c_ones": ones, "c_grid": np.concatenate([grid, own], 1), "c_ident": np.eye(P, dtype=np.float32)}


def at(i, per, c):
    reg, off, step = i
    return per * off + c if reg is None else reg * (per * step) + (per * off + c)


def wait(eng, sem, i, per, c):
    v = at(i, per, c)
    if i[0] is not None or v > 0:
        eng.wait_ge(sem, v)


def xattn_kernel(nc, x, ctx, bbox, w_q, w_k, w_v, w_k_ip, w_v_ip, w_out, b_out,
                 c_sel, c_ones, c_grid, c_ident, out, NB):
    k_scratch = nc.dram_tensor("k_scratch", (NB, 3 * P, 2, KEYS), fp32, kind="Internal").ap()
    v_scratch = nc.dram_tensor("v_scratch", (NB, H, KEYS, 3 * DH), bf16, kind="Internal").ap()

    ctx_stack = ExitStack()
    with ctx_stack:
        def sb(name, shape, dt, stack=ctx_stack):
            return stack.enter_context(nc.sbuf_tensor(name, shape, dt))

        def sem(name):
            return ctx_stack.enter_context(nc.semaphore(name))

        ident = sb("ident", [P, P], fp32)
        grid = sb("grid", [P, 4 + H], fp32)
        own = grid[:, 4:4 + H]
        own_rows = sb("own_rows", [P, TILES, SLOTS * (SLOT - 2)], bf16)
        wq = [sb(f"wq_{n}", [P, 3, 384], f32r) for n in ("hi", "lo")]
        wo = [sb(f"wo_{n}", [P, 3, D], f32r) for n in ("hi", "lo")]
        sel = sb("sel", [P, ROWS], f32r)
        mask = sb("mask", [P, NT, NB * NIP], fp32)
        bias = sb("bias", [P, D], fp32)
        values = [sb(f"values{q}", [P, VCOLS], bf16) for q in range(2)]
        keys = [[sb(f"keys_{n}{q}", [P, ROWS], f32r) for n in ("hi", "lo")] for q in range(2)]
        raw_v = [sb(f"raw_v{q}", [P, TILES, 3 * DH], bf16) for q in range(2)]

        with ExitStack() as st:
            raw_q = sb("raw_q", [P, 3, 384], fp32, st)
            raw_o = sb("raw_o", [P, 3, D], fp32, st)
            raw_w = [sb(f"raw_w{n}", [P, KC, D], fp32, st) for n in range(4)]
            raw_c = sb("raw_c", [P, VCOLS], fp32, st)
            box = sb("box", [P, NB, 4, 4], fp32, st)
            inside = [sb(f"inside{n}", [P, NB, 4], fp32, st) for n in range(4)]
            anyin = sb("anyin", [P, NB], fp32, st)
            ctx_in = [sb(f"ctx_in{j}", [KEYS, C], fp32, st) for j in range(CB)]
            ctxT = [sb(f"ctxT_{n}", [P, KC, CB, CK], f32r, st) for n in ("hi", "lo")]
            ipT = [sb(f"ipT_{n}", [P, KC, CB * NIP], f32r, st) for n in ("hi", "lo")]
            w_hi = [sb(f"w_hi{n}", [P, KC, D], f32r, st) for n in range(4)]
            w_lo = [sb(f"w_lo{n}", [P, KC, D], f32r, st) for n in range(4)]
            k_stage = [sb(f"k_stage{m}", [P, 2, CB, KEYS], f32r, st) for m in range(3)]
            v_stage = [sb(f"v_stage{n}", [T, H, 3, DH], bf16, st) for n in range(3)]
            v_rest = [sb(f"v_rest{n}", [T, D], fp32, st) for n in range(3)]
            ps_t = [st.enter_context(nc.psum_tensor(f"ps_t{n}", [P, 512], fp32)) for n in range(2)]
            ps_k = [st.enter_context(nc.psum_tensor(f"ps_k{n}", [P, 512], fp32)) for n in range(3)]
            ps_v = [st.enter_context(nc.psum_tensor(f"ps_v{n}", [P, 512], fp32)) for n in range(3)]
            VBUF = [0, 1, 0, 1, 2]

            s_const = sem("constants_loaded")
            s_w = sem("weights_loaded")
            s_w2 = sem("main_weights_loaded")
            s_ctx = [sem(f"context_loaded{j}") for j in range(CB)]
            s_setup = sem("setup_steps")
            s_zero = sem("zeroed")
            s_wsplit = sem("weights_split")
            s_t = sem("context_transposed")
            s_chi = sem("context_hi")
            s_clo = sem("context_lo")
            s_k = sem("keys_projected")
            s_khi = sem("keys_hi")
            s_klo = sem("keys_lo")
            s_v = sem("values_projected")
            s_vhi = sem("values_hi")
            s_vrest = sem("values_rest")
            s_vmid = sem("values_middle")
            s_vlo = sem("values_lo")
            s_kst = [sem(f"keys_stored{m}") for m in range(3)]
            s_vst = [sem(f"values_stored{n}") for n in range(3)]
            WN = (w_k, w_k_ip, w_v, w_v_ip)
            KW = [128, 128, 64]
            NI = NB // CB

            def steps(eng, body):
                body(eng, (None, 0, 1))
                if NI > 1:
                    with eng.Fori(1, NI) as i:
                        body(eng, (i, 0, 1))

            with nc.Block() as block:

                @block.sync
                def _(sp):
                    sp.dma_start(ident[:], c_ident).then_inc(s_const, 16)
                    for n in range(4):
                        sp.dma_start(raw_w[n][:], WN[n].rearrange("(k p) n -> p k n", p=P)).then_inc(s_w, 16)

                    def body(sp, i):
                        for j in range(CB):
                            wait(sp, s_t, i, CB, j + 1 - CB)
                            n = at(i, CB, j)
                            sp.dma_start(ctx_in[j][:], ctx[bass.ds(n, 1), :, :].rearrange("a k c -> (a k) c")
                                         ).then_inc(s_ctx[j], 16)
                        if i[0] is None:
                            for k in range(2):
                                sp.dma_start(raw_q[:, k, 0:D], w_q[k * P:(k + 1) * P, :]).then_inc(s_w2, 16)
                                sp.dma_start(raw_q[:, k, D:384], w_q[k * P:(k + 1) * P, 256:D]).then_inc(s_w2, 16)
                                sp.dma_start(raw_q[64 * k:64 * k + 64, 2, 0:D], w_q[256:D, :]).then_inc(s_w2, 16)
                                sp.dma_start(raw_q[64 * k:64 * k + 64, 2, D:384], w_q[256:D, 256:D]).then_inc(s_w2, 16)
                                sp.dma_start(raw_o[:, k, :], w_out[k * P:(k + 1) * P, :]).then_inc(s_w2, 16)
                                sp.dma_start(raw_o[64 * k:64 * k + 64, 2, :], w_out[256:D, :]).then_inc(s_w2, 16)
                            sp.dma_start(grid[:], c_grid).then_inc(s_w2, 16)
                            sp.dma_start(box[:].rearrange("p b m c -> p (b m c)"),
                                         bbox.rearrange("b m c -> (b m c)").partition_broadcast(P)).then_inc(s_w2, 16)
                            sp.dma_start(bias[:], b_out.partition_broadcast(P)).then_inc(s_w2, 16)
                            sp.dma_start(raw_c[:, 0:VCOLS], c_ones).then_inc(s_w2, 16)
                        for u in range(CB):
                            sp.wait_ge(s_vlo, at(i, 5, u + 1))
                            n = at(i, CB, u)
                            sp.dma_start(v_scratch[bass.ds(n, 1), :, 0:T, :].rearrange("a h k c -> (a k) h c"),
                                         v_stage[VBUF[u]][:].rearrange("k h s c -> k h (s c)")
                                         ).then_inc(s_vst[VBUF[u]], 16)
                        sp.wait_ge(s_vlo, at(i, 5, 5))
                        for j in range(CB):
                            n = at(i, CB, j)
                            sp.dma_start(v_scratch[bass.ds(n, 1), :, T:KEYS, :].rearrange("a h k c -> (a k) h c"),
                                         v_stage[2][NIP * j:NIP * (j + 1)].rearrange("k h s c -> k h (s c)")
                                         ).then_inc(s_vst[2], 16)
                        for m in range(3):
                            sp.wait_ge(s_klo, at(i, 3, m + 1))
                            n = at(i, CB, 0)
                            for h in range(2):
                                for r0 in (m * P, m * P + 64)[0:1 + m // 2]:
                                    sp.dma_start(
                                        k_scratch[bass.ds(n, CB), r0:r0 + KW[m], h, :].rearrange("j p k -> p j k"),
                                        k_stage[m][0:KW[m], h].bitcast(fp32)).then_inc(s_kst[m], 16)

                    steps(sp, body)
                    sp.wait_ge(s_wsplit, 8)
                    sp.wait_ge(s_setup, 4 + 3)
                    sp.dma_start(raw_c[:, 0:ROWS], c_sel).then_inc(s_const, 16)
                    for m in range(3):
                        sp.wait_ge(s_kst[m], (32 if m < 2 else 64) * NI)
                    for n in range(3):
                        sp.wait_ge(s_vst[n], (32 if n < 2 else 64) * NI)

                @block.tensor
                def _(pe):
                    pe.wait_ge(s_const, 16)

                    def three(ps, stat, mov, skip=False, first=True):
                        for k in range(KC):
                            for n, (a, b) in enumerate(((0, 0), (0, 1), (1, 0))):
                                last = nc.tensor.matmul(ps, stat(a, k), mov(b, k), start=first and k == 0 and n == 0,
                                                        stop=k == KC - 1 and n == 2, skip_group_check=skip)
                        return last

                    def body(pe, i):
                        for j in range(CB):
                            pe.wait_ge(s_ctx[j], at(i, 16, 16))
                            wait(pe, s_clo, i, CB, j - 1)
                            for k in range(KC):
                                last = nc.tensor.transpose(ps_t[j % 2][:, k * KEYS:(k + 1) * KEYS],
                                                           ctx_in[j][:, k * P:(k + 1) * P], ident[0:KEYS, 0:KEYS])
                            last.then_inc(s_t, 1)
                        if i[0] is None:
                            pe.wait_ge(s_wsplit, 4)
                        for u in range(5):
                            pe.wait_ge(s_clo, at(i, CB, min(u + 1, CB)))
                            wait(pe, s_vrest, i, 5, u - 1 if u >= 2 and u < 4 else [-2, -1, 0, 0, 0][u])
                            if u < CB:
                                last = three(ps_v[VBUF[u]][0:T, 0:D], lambda a, k: ctxT[a][:, k, u, 0:T],
                                             lambda b, k: (w_hi, w_lo)[b][2][:, k, :])
                            else:
                                last = three(ps_v[2][0:CB * NIP, 0:D], lambda a, k: ipT[a][:, k, :],
                                             lambda b, k: (w_hi, w_lo)[b][3][:, k, :])
                            last.then_inc(s_v, 1)
                        for m in range(3):
                            wait(pe, s_klo, i, 3, m - 2)
                            cols = slice(m * P, m * P + KW[m])
                            three(ps_k[m][0:KW[m], 0:CB * CK], lambda a, k: (w_hi, w_lo)[a][0][:, k, cols],
                                  lambda b, k: ctxT[b][:, k].rearrange("p j k -> p (j k)"), skip=True)
                            last = three(ps_k[m][0:KW[m], CB * CK:CB * CK + CB * NIP],
                                         lambda a, k: (w_hi, w_lo)[a][1][:, k, cols],
                                         lambda b, k: ipT[b][:, k, :], skip=True, first=False)
                            last.then_inc(s_k, 1)

                    steps(pe, body)

                @block.scalar
                def _(act):
                    act.wait_ge(s_zero, 1)

                    def v_hi(i, u):
                        act.wait_ge(s_v, at(i, 5, u + 1))
                        if u < CB:
                            wait(act, s_vst[VBUF[u]], i, 32, 16 * (u // 2))
                        else:
                            wait(act, s_vst[2], i, 64, 0)
                        n, r = VBUF[u], (T if u < CB else CB * NIP)
                        nc.scalar.copy(v_stage[n][0:r, :, 0, :],
                                       ps_v[n][0:r, 0:D].rearrange("p (h c) -> p h c", c=DH)).then_inc(s_vhi, 1)

                    def v_mid(i, u):
                        act.wait_ge(s_vrest, at(i, 5, u + 1))
                        n, r = VBUF[u], (T if u < CB else CB * NIP)
                        nc.scalar.copy(v_stage[n][0:r, :, 1, :],
                                       v_rest[n][0:r, :].rearrange("p (h c) -> p h c", c=DH)).then_inc(s_vmid, 1)

                    def k_hi(i, m):
                        act.wait_ge(s_k, at(i, 3, m + 1))
                        wait(act, s_kst[m], i, 32 if m < 2 else 64, 0)
                        w = KW[m]
                        nc.scalar.mul(k_stage[m][0:w, 0, :, 0:T],
                                      ps_k[m][0:w, 0:CB * CK].rearrange("p (j k) -> p j k", j=CB)[:, :, 0:T], 0.25)
                        nc.scalar.mul(k_stage[m][0:w, 0, :, T:KEYS],
                                      ps_k[m][0:w, CB * CK:CB * (CK + NIP)].rearrange("p (j k) -> p j k", j=CB),
                                      0.25).then_inc(s_khi, 1)

                    def body(act, i):
                        for j in range(CB):
                            act.wait_ge(s_t, at(i, CB, j + 1))
                            if j == 0:
                                wait(act, s_k, i, 3, 0)
                            ps = ps_t[j % 2][:, 0:KC * KEYS].rearrange("p (k n) -> p k n", k=KC)
                            nc.scalar.copy(ctxT[0][:, :, j, 0:T], ps[:, :, 0:T])
                            nc.scalar.copy(ipT[0][:, :, NIP * j:NIP * (j + 1)], ps[:, :, T:KEYS]).then_inc(s_chi, 1)
                        v_hi(i, 0)
                        for u in range(1, 5):
                            v_hi(i, u)
                            v_mid(i, u - 1)
                        k_hi(i, 0)
                        v_mid(i, 4)
                        k_hi(i, 1)
                        k_hi(i, 2)

                    steps(act, body)

                @block.vector
                def _(dve):
                    n_setup = [0]

                    def then(ins):
                        n_setup[0] += 1
                        ins.then_inc(s_setup, 1)
                        dve.wait_ge(s_setup, n_setup[0])

                    for a in ctxT:
                        last = nc.vector.memset(a[:].bitcast(fp32), 0.0)
                    last.then_inc(s_zero, 1)
                    dve.wait_ge(s_w, 16 * 4)
                    for n in (2, 3, 0, 1):
                        then(nc.vector.tensor_copy(w_hi[n][:], raw_w[n][:]))
                        nc.vector.tensor_tensor(w_lo[n][:], raw_w[n][:], w_hi[n][:].bitcast(fp32),
                                                ALU.subtract).then_inc(s_wsplit, 1)

                    def body(dve, i):
                        for j in range(CB):
                            dve.wait_ge(s_chi, at(i, CB, j + 1))
                            ps = ps_t[j % 2][:, 0:KC * KEYS].rearrange("p (k n) -> p k n", k=KC)
                            ip = slice(NIP * j, NIP * (j + 1))
                            nc.vector.tensor_tensor(ctxT[1][:, :, j, 0:T], ps[:, :, 0:T],
                                                    ctxT[0][:, :, j, 0:T].bitcast(fp32), ALU.subtract)
                            nc.vector.tensor_tensor(ipT[1][:, :, ip], ps[:, :, T:KEYS],
                                                    ipT[0][:, :, ip].bitcast(fp32), ALU.subtract).then_inc(s_clo, 1)
                        for u in range(5):
                            dve.wait_ge(s_vhi, at(i, 5, u + 1))
                            n, r = VBUF[u], (T if u < CB else CB * NIP)
                            nc.vector.tensor_tensor(v_rest[n][0:r, :].rearrange("p (h c) -> p h c", c=DH),
                                                    ps_v[n][0:r, 0:D].rearrange("p (h c) -> p h c", c=DH),
                                                    v_stage[n][0:r, :, 0, :], ALU.subtract).then_inc(s_vrest, 1)
                        for m in range(3):
                            dve.wait_ge(s_khi, at(i, 3, m + 1))
                            w = KW[m]
                            nc.vector.scalar_tensor_tensor(
                                out=k_stage[m][0:w, 1, :, 0:T],
                                in0=ps_k[m][0:w, 0:CB * CK].rearrange("p (j k) -> p j k", j=CB)[:, :, 0:T],
                                scalar=0.25, in1=k_stage[m][0:w, 0, :, 0:T].bitcast(fp32),
                                op0=ALU.mult, op1=ALU.subtract)
                            nc.vector.scalar_tensor_tensor(
                                out=k_stage[m][0:w, 1, :, T:KEYS],
                                in0=ps_k[m][0:w, CB * CK:CB * (CK + NIP)].rearrange("p (j k) -> p j k", j=CB),
                                scalar=0.25, in1=k_stage[m][0:w, 0, :, T:KEYS].bitcast(fp32),
                                op0=ALU.mult, op1=ALU.subtract).then_inc(s_klo, 1)

                    steps(dve, body)

                    dve.wait_ge(s_w2, 16 * (12 + 4))
                    then(nc.vector.tensor_copy(wq[0][:], raw_q[:]))
                    then(nc.vector.tensor_copy(wo[0][:], raw_o[:]))
                    nc.vector.tensor_tensor(wq[1][:], raw_q[:], wq[0][:].bitcast(fp32), ALU.subtract).then_inc(s_wsplit, 1)
                    nc.vector.tensor_tensor(wo[1][:], raw_o[:], wo[0][:].bitcast(fp32), ALU.subtract).then_inc(s_wsplit, 1)
                    for q in range(2):
                        for a in keys[q]:
                            nc.vector.memset(a[:].bitcast(fp32), 0.0)
                        nc.vector.memset(raw_v[q][:], 0.0)
                        nc.vector.tensor_copy(values[q][:], raw_c[:, 0:VCOLS]).then_inc(s_wsplit, 1)
                    then(nc.vector.tensor_copy(
                        own_rows[:].rearrange("p t (n c) -> p (t n) c", n=SLOTS),
                        raw_c[:, 0:VCOLS].rearrange("p (n c) -> p n c", c=SLOT)[:, :, 2:SLOT]))
                    for t in range(NT):
                        xg, yg = grid[:, 0:1], grid[:, 1 + t:2 + t]
                        then(nc.vector.tensor_scalar(inside[0][:], box[:, :, :, 0], xg, None, ALU.is_le))
                        for n, c, g, op in ((1, 2, xg, ALU.is_ge), (2, 1, yg, ALU.is_le), (3, 3, yg, ALU.is_ge)):
                            then(nc.vector.scalar_tensor_tensor(out=inside[n][:], in0=box[:, :, :, c], scalar=g,
                                                                in1=inside[n - 1][:], op0=op, op1=ALU.mult))
                        then(nc.vector.tensor_reduce(anyin[:], inside[3][:], AX.X, ALU.max))
                        mt = mask[:, t, :].rearrange("p (b k) -> p b k", k=NIP)
                        nc.vector.tensor_scalar(mt[:, :, 4:8], inside[3][:], -NEG, NEG, ALU.mult, ALU.add)
                        then(nc.vector.tensor_scalar(mt[:, :, 0:4], anyin[:].rearrange("p (b o) -> p b o", o=1).broadcast_to([P, NB, 4]),
                                                     NEG, None, ALU.mult))
                    dve.wait_ge(s_const, 32)
                    then(nc.vector.tensor_copy(sel[:], raw_c[:, 0:ROWS]))

                @block.gpsimd
                def _(pool):
                    def body(pool, i):
                        for u in range(5):
                            pool.wait_ge(s_vmid, at(i, 5, u + 1))
                            n, r = VBUF[u], (T if u < CB else CB * NIP)
                            nc.gpsimd.tensor_tensor(v_stage[n][0:r, :, 2, :],
                                                    v_rest[n][0:r, :].rearrange("p (h c) -> p h c", c=DH),
                                                    v_stage[n][0:r, :, 1, :], ALU.subtract).then_inc(s_vlo, 1)
                    steps(pool, body)

        with ExitStack() as st:
            raw_k = [sb(f"raw_k{q}", [P, 3, 2, KEYS], fp32, st) for q in range(2)]
            x_in = [sb(f"x_in{q}", [P, NT, DW], fp32, st) for q in range(2)]
            x_bias = [sb(f"x_bias{q}", [P, NT, D], fp32, st) for q in range(2)]
            y = [sb(f"y{q}", [P, NT, D], fp32, st) for q in range(2)]
            xT = [sb(f"xT_{n}", [P, 2, S], f32r, st) for n in ("hi", "lo")]
            xT2 = sb("xT2", [P, S], f32r, st)
            qT = [[sb(f"qT_{n}{q}", [P, 2, S], f32r, st) for n in ("hi", "lo")] for q in range(2)]
            qT2 = [sb(f"qT2_{q}", [P, S], f32r, st) for q in range(2)]
            stats = sb("stats", [P, NT, P], fp32, st)
            extra = sb("extra", [P, S], f32r, st)
            ip_masked = [sb(f"ip_masked{n}", [P, 4, NIP], fp32, st) for n in range(2)]
            prob = sb("prob", [P, PAIRS, 2 * S], fp32, st)
            prob_hi = [sb(f"prob_hi{q}", [P, PAIRS, 2 * S], fp16, st) for q in range(2)]
            prob_lo = [sb(f"prob_lo{q}", [P, PAIRS, 2 * S], fp16, st) for q in range(2)]
            inv = sb("inv", [P, 16], fp32, st)
            heads = [sb(f"heads{n}", [P, 16, DH], fp32, st) for n in range(2)]
            attn = sb("attn", [P, NT, DW], fp32, st)
            aT = [sb(f"aT_{n}", [P, 2, S], f32r, st) for n in ("hi", "lo")]
            aT2 = sb("aT2", [P, S], f32r, st)
            ps_s = [st.enter_context(nc.psum_tensor(f"ps_s{n}", [P, 512], fp32)) for n in range(3)]
            ps_m = [st.enter_context(nc.psum_tensor(f"ps_m{n}", [P, 512], fp32)) for n in range(2)]
            ps_o = st.enter_context(nc.psum_tensor("ps_o", [P, 512], fp32))
            ps_a = st.enter_context(nc.psum_tensor("ps_a", [P, 512], fp32))
            ps_b = st.enter_context(nc.psum_tensor("ps_b", [P, 512], fp32))

            s_x = [sem(f"x_loaded{q}") for q in range(2)]
            s_keys = [sem(f"keys_loaded{q}") for q in range(2)]
            s_vals = [sem(f"values_loaded{q}") for q in range(2)]
            s_kx = [sem(f"keys_{n}_spread") for n in ("hi", "lo")]
            s_vx = sem("values_spread")
            s_y = [sem(f"y_stored{q}") for q in range(2)]
            s_xt = sem("x_transposed")
            s_xhi = sem("xT_hi_ready")
            s_xlo = sem("xT_ready")
            s_q = sem("q_projected")
            s_qhi = sem("qT_hi_ready")
            s_qlo = sem("qT_ready")
            s_mps = sem("max_scores")
            s_mx = sem("max_found")
            s_dve = sem("masked_ip_ready")
            s_mk = sem("mask_in_stats")
            s_et = sem("stats_transposed")
            s_ex = sem("extra_ready")
            s_sc = sem("scores_ready")
            s_hi = sem("probs_hi_ready")
            s_lo = sem("probs_lo_ready")
            s_pv = sem("heads_summed")
            s_inv = sem("inverse_ready")
            s_nm = sem("heads_normed")
            s_at = sem("attn_ready")
            s_att = sem("attn_transposed")
            s_ahi = sem("aT_hi_ready")
            s_alo = sem("aT_ready")
            s_op = sem("out_projected")
            s_yr = sem("y_ready")
            s_xb = sem("x_bias_ready")
            s_z = sem("stats_zeroed")

            def sched(eng, step):
                first, last = min(2, NB), max(NB - 2, min(2, NB))
                last -= (last - first) % 2
                for b in range(-1, first):
                    step(eng, (None, b, 1), b)
                if last > first:
                    with eng.Fori(0, (last - first) // 2) as i:
                        for o in range(2):
                            step(eng, (i, first + o, 2), None)
                for b in range(last, NB + 1):
                    step(eng, (None, b, 1), b)

            def par(b):
                return b[1] % 2

            def nth(b, per, c=0):
                reg, off, stp = b
                return per * (off // 2 + 1) + c if reg is None else reg * (per * stp // 2) + (per * (off // 2 + 1) + c)

            def off(b, n):
                return (b[0], b[1] + n, b[2])

            def has(n):
                return (True, True, True) if n is None else (n + 1 < NB, 0 <= n < NB, n >= 1)

            def quad_cols(h4):
                g = h4 // 2 if h4 < 4 else 2
                c = GTILE[g] * P + (h4 % 2 if h4 < 4 else 0) * QUAD
                return g, slice(c, c + QUAD)

            def spread_keys(eng, b, half):
                for g, heads in enumerate(GROUPS):
                    c = GTILE[g] * P
                    last = eng.tensor_tensor(
                        keys[par(b)][half][:, c:c + heads * KEYS].rearrange("p (h k) -> p h k", k=KEYS),
                        raw_k[par(b)][:, g, half:half + 1, :].broadcast_to([P, heads, KEYS]),
                        own[:, GHEAD[g]:GHEAD[g] + heads].rearrange("p (h o) -> p h o", o=1).broadcast_to([P, heads, KEYS]),
                        ALU.mult)
                last.then_inc(s_kx[half], 1)

            with nc.Block() as block:

                @block.sync
                def _(sp):
                    def load_x(b):
                        xb = x[bass.ds(at(b, 1, 0), 1), :, :].rearrange("a (t p) d -> (a p) t d", p=P)
                        sp.dma_start(x_in[par(b)][:, :, 0:D], xb).then_inc(s_x[par(b)], 16)
                        sp.dma_start(x_in[par(b)][:, :, D:DW], xb[:, :, 256:D]).then_inc(s_x[par(b)], 16)

                    def load_keys(b):
                        sp.dma_start(raw_k[par(b)][:], k_scratch[bass.ds(at(b, 1, 0), 1), :, :, :]
                                     .rearrange("a (g p) s k -> (a p) g s k", p=P)).then_inc(s_keys[par(b)], 16)

                    def load_values(b):
                        for g, heads in enumerate(GROUPS):
                            src = v_scratch[bass.ds(at(b, 1, 0), 1), GHEAD[g]:GHEAD[g] + heads, :, :].rearrange("a h k c -> (a h k) c")
                            full, rest = GTILES[g] - 1, heads * KEYS - (GTILES[g] - 1) * P
                            sp.dma_start(raw_v[par(b)][:, GTILE[g]:GTILE[g] + full, :],
                                         src[0:full * P, :].rearrange("(t p) c -> p t c", p=P)).then_inc(s_vals[par(b)], 16)
                            sp.dma_start(raw_v[par(b)][0:rest, GTILE[g] + full, :],
                                         src[full * P:full * P + rest, :]).then_inc(s_vals[par(b)], 16)

                    def step(sp, b, n):
                        A, Bs, Cs = has(n)
                        if n == -1:
                            for b in range(min(2, NB)):
                                load_x((None, b, 1))
                                load_keys((None, b, 1))
                                load_values((None, b, 1))
                            return
                        if n is None or n + 2 < NB:
                            sp.wait_ge(s_xt, at(b, NT, NT))
                            sp.wait_ge(s_xb, at(b, 1, 1))
                            load_x(off(b, 2))
                            for m in range(2):
                                sp.wait_ge(s_kx[m], at(b, 1, 1))
                            load_keys(off(b, 2))
                            sp.wait_ge(s_vx, at(b, 1, 1))
                            load_values(off(b, 2))
                        if Cs:
                            c = off(b, -1)
                            for t in range(NT):
                                sp.wait_ge(s_yr, at(c, NT, t + 1))
                                sp.dma_start(out[bass.ds(at(c, 1, 0), 1), t * P:(t + 1) * P, :].rearrange("a p d -> (a p) d"),
                                             y[par(c)][:, t, :]).then_inc(s_y[par(c)], 16)

                    sched(sp, step)
                    for q in range(2):
                        if NB > q:
                            sp.wait_ge(s_y[q], 32 * ((NB - q + 1) // 2))

                @block.tensor
                def _(pe):
                    mm = nc.tensor.matmul

                    def x_transpose(b, t, n):
                        if t == 0:
                            pe.wait_ge(s_x[par(b)], nth(b, 32))
                            if n is None or n >= 2:
                                pe.wait_ge(s_yr, at(b, NT, -2 * NT))
                            elif n >= 0:
                                pe.wait_ge(s_qlo, at(b, 3, 0))
                        else:
                            wait(pe, s_ex, b, 1, 0)
                        ps = (ps_a, ps_b)[t]
                        for k in range(2):
                            nc.tensor.transpose(ps[:, k * P:(k + 1) * P], x_in[par(b)][:, t, k * P:(k + 1) * P], ident[:])
                        nc.tensor.transpose(ps[:, 2 * P:3 * P], x_in[par(b)][:, t, 256:DW], ident[:]).then_inc(s_xt, 1)

                    def split_product(ps, hi, lo, both, w, cols, swap):
                        terms = []
                        for k in range(2):
                            terms += [(hi(k), w[0][:, k, cols]), (hi(k), w[1][:, k, cols]), (lo(k), w[0][:, k, cols])]
                        terms += [(both, w[0][:, 2, cols]), (both, w[1][:, 2, cols])]
                        for n, (a, ww) in enumerate(terms):
                            last = mm(ps, ww if swap else a, a if swap else ww, start=n == 0, stop=n == len(terms) - 1)
                        return last

                    def project(b, m):
                        if m == 0:
                            pe.wait_ge(s_xlo, at(b, NT, NT))
                        if m == 2:
                            pe.wait_ge(s_qlo, at(b, 3, 1))
                        ps = (ps_a, ps_b)[m % 2]
                        split_product(ps[:, 0:S], lambda k: xT[0][:, k, :], lambda k: xT[1][:, k, :], xT2[:, :],
                                      wq, slice(m * P, (m + 1) * P), True).then_inc(s_q, 1)

                    def max_scores(b, n):
                        h4, t = n // NT, n % NT
                        g, cols = quad_cols(h4)
                        pe.wait_ge(s_qlo, at(b, 3, g + 1)) if n % 4 == 0 else None
                        if n == 0:
                            pe.wait_ge(s_kx[0], at(b, 1, 1))
                        wait(pe, s_mx, b, NT * QUADS, n - 1)
                        stat = qT[par(b)][0][:, g, t * P:(t + 1) * P] if g < 2 else qT2[par(b)][:, t * P:(t + 1) * P]
                        mm(ps_m[n % 2][:, 0:QUAD], stat, keys[par(b)][0][:, cols], start=True, stop=True).then_inc(s_mps, 1)

                    def stats_transpose(b, n):
                        pe.wait_ge(s_mx, at(b, NT * QUADS, NT * QUADS))
                        if n is None or n >= 1:
                            pe.wait_ge(s_alo, at(b, NT, -NT))
                        else:
                            pe.wait_ge(s_qlo, at(b, 3, 2))
                        for t in range(NT):
                            last = nc.tensor.transpose(ps_b[:, t * P:(t + 1) * P], stats[:, t, :], ident[:])
                        last.then_inc(s_et, 1)

                    def scores(b, s):
                        wait(pe, s_hi, b, PAIRS, [-3, 0, -1, 1, 2, 3, 5][s])
                        if s == 0:
                            pe.wait_ge(s_kx[1], at(b, 1, 1))
                        q = par(b)
                        for o, t in enumerate(range(2 * s, min(2 * s + 2, TILES))):
                            ps = ps_s[RING[s]][:, o * S:(o + 1) * S]
                            g = PARTS[t][0]
                            c = slice(t * P, (t + 1) * P)
                            if g < 2:
                                mm(ps, keys[q][0][:, c], qT[q][0][:, g, :], start=True, stop=False)
                                mm(ps, keys[q][0][:, c], qT[q][1][:, g, :], start=False, stop=False)
                                mm(ps, keys[q][1][:, c], qT[q][0][:, g, :], start=False, stop=False)
                            else:
                                mm(ps, keys[q][0][:, c], qT2[q][:, :], start=True, stop=False)
                                mm(ps, keys[q][1][:, c], qT2[q][:, :], start=False, stop=False)
                            if t == 0:
                                pe.wait_ge(s_ex, at(b, 1, 1))
                            last = mm(ps, sel[:, c], extra[:, :], start=False, stop=True)
                        last.then_inc(s_sc, 1)

                    def sum_heads(b, u):
                        t, g = u // 3, u % 3
                        q = par(b)
                        if u == 0:
                            pe.wait_ge(s_vx, at(b, 1, 1))
                        if t == 0:
                            pe.wait_ge(s_lo, at(b, PAIRS, (3, 5, 7)[g]))
                        wait(pe, s_nm, b, UNITS, u)
                        first = True
                        for tt in range(GTILE[g], GTILE[g] + GTILES[g]):
                            s0, ns = PARTS[tt][1], NSLOTS[tt]
                            c = (tt % 2) * S + t * P
                            v = values[q][:, tt * SLOTS * SLOT:(tt * SLOTS + ns) * SLOT].rearrange("p (n c) -> p n c", c=SLOT)
                            o = ps_o[:, s0 * 17:(s0 + ns) * 17].rearrange("p (n c) -> p n c", c=17)
                            for pr, parts in ((prob_hi, 3), (prob_lo, 2)):
                                stat = pr[q][:, tt // 2, c:c + P]
                                for part in range(parts):
                                    a, w, oo = (1, 17, 0) if part == 0 else (2 + 16 * part, 16, 1)
                                    last = mm(o[:, :, oo:oo + w], stat, v[:, :, a:a + w], start=first, stop=False,
                                              skip_group_check=True)
                                    first = False
                        last.then_inc(s_pv, 1)

                    def attn_transpose(b, t, A, n):
                        pe.wait_ge(s_at, at(b, UNITS, 3 * t + 3))
                        if t == 1:
                            pe.wait_ge(s_alo, at(b, NT, 1))
                        elif A:
                            pe.wait_ge(s_qlo, at(b, 3, 3 * 2 + 2))
                        elif n == NB - 1:
                            pe.wait_ge(s_ex, NB)
                        else:
                            wait(pe, s_alo, b, NT, 0)
                        for k in range(2):
                            nc.tensor.transpose(ps_b[:, k * P:(k + 1) * P], attn[:, t, k * P:(k + 1) * P], ident[:])
                        nc.tensor.transpose(ps_b[:, 2 * P:3 * P], attn[:, t, 256:DW], ident[:]).then_inc(s_att, 1)

                    def project_out(b, t, A):
                        pe.wait_ge(s_alo, at(b, NT, t + 1))
                        if t == 0 and A:
                            pe.wait_ge(s_qlo, at(b, 3, 3 * 2 + 3))
                        else:
                            wait(pe, s_yr, b, NT, t)
                        c = slice(t * P, (t + 1) * P)
                        split_product(ps_a[:, 0:D], lambda k: aT[0][:, k, c], lambda k: aT[1][:, k, c], aT2[:, c],
                                      wo, slice(0, D), False).then_inc(s_op, 1)

                    def step(pe, b, n):
                        A, Bs, Cs = has(n)
                        a, c = off(b, 1), off(b, -1)
                        for s in range(PAIRS):
                            if Bs:
                                scores(b, s)
                            if A:
                                if s < 2:
                                    x_transpose(a, s, n)
                                elif s < 5:
                                    project(a, s - 2)
                                if s >= 3:
                                    for m in ([0], [1], [2, 3], [4, 5, 6])[s - 3]:
                                        max_scores(a, m)
                            if Cs:
                                if s == 4:
                                    attn_transpose(c, 0, A, n)
                                if s == 5:
                                    project_out(c, 0, A)
                                if s < UNITS:
                                    sum_heads(c, s)
                                if s == 6:
                                    attn_transpose(c, 1, A, n)
                        if A:
                            for m in (7, 8, 9):
                                max_scores(a, m)
                        if Cs:
                            project_out(c, 1, A)
                        if A:
                            stats_transpose(a, n)

                    sched(pe, step)

                @block.scalar
                def _(act):
                    def step(act, b, n):
                        A, Bs, Cs = has(n)
                        a, c = off(b, 1), off(b, -1)

                        def x_hi(t):
                            act.wait_ge(s_xt, at(a, NT, t + 1))
                            ps = (ps_a, ps_b)[t]
                            cols = slice(t * P, (t + 1) * P)
                            nc.scalar.copy(xT[0][:, :, cols], ps[:, 0:2 * P].rearrange("p (k s) -> p k s", k=2))
                            nc.scalar.copy(xT2[0:64, cols], ps[0:64, 2 * P:3 * P]).then_inc(s_xhi, 1)

                        def q_hi(m):
                            act.wait_ge(s_q, at(a, 3, m + 1))
                            ps = (ps_a, ps_b)[m % 2]
                            if m < 2:
                                nc.scalar.copy(qT[par(a)][0][:, m, :], ps[:, 0:S]).then_inc(s_qhi, 1)
                            else:
                                nc.scalar.copy(qT2[par(a)][0:64, :], ps[0:64, 0:S]).then_inc(s_qhi, 1)

                        def a_hi(t):
                            act.wait_ge(s_att, at(c, NT, t + 1))
                            cols = slice(t * P, (t + 1) * P)
                            nc.scalar.copy(aT[0][:, :, cols], ps_b[:, 0:2 * P].rearrange("p (k s) -> p k s", k=2))
                            nc.scalar.copy(aT2[0:64, cols], ps_b[0:64, 2 * P:3 * P]).then_inc(s_ahi, 1)

                        for s in range(PAIRS):
                            if Bs:
                                act.wait_ge(s_sc, at(b, PAIRS, s + 1))
                                wait(act, s_lo, b, PAIRS, s + 1 - PAIRS)
                                w = S * (2 if 2 * s + 1 < TILES else 1)
                                nc.scalar.activation(prob[:, s, 0:w], ps_s[RING[s]][:, 0:w], ACT.Exp)
                                nc.scalar.activation(prob_hi[par(b)][:, s, 0:w], ps_s[RING[s]][:, 0:w], ACT.Exp
                                                     ).then_inc(s_hi, 1)
                            if A:
                                if s < 2:
                                    x_hi(s)
                                elif s < 5:
                                    q_hi(s - 2)
                            if Cs and s in (4, 6):
                                a_hi((s - 4) // 2)
                        if A:
                            act.wait_ge(s_et, at(a, 1, 1))
                            nc.scalar.copy(extra[:, :], ps_b[:, 0:S]).then_inc(s_ex, 1)

                    sched(act, step)

                @block.vector
                def _(dve):
                    nc.vector.memset(stats[:], 0.0).then_inc(s_z, 1)
                    dve.wait_ge(s_z, 1)
                    nc.vector.memset(stats[:, :, R_ONE:R_ONE + 1], SHIFT).then_inc(s_z, 1)
                    dve.wait_ge(s_z, 2)

                    def step(dve, b, n):
                        A, Bs, Cs = has(n)
                        a, c = off(b, 1), off(b, -1)

                        def low(dst, dst2, ps, hi, hi2, sem_, w):
                            nc.vector.tensor_tensor(dst, ps[:, 0:2 * P].rearrange("p (k s) -> p k s", k=2),
                                                    hi.bitcast(fp32), ALU.subtract)
                            nc.vector.tensor_tensor(dst2, ps[64:P, 2 * P:3 * P], hi2.bitcast(fp32),
                                                    ALU.subtract).then_inc(sem_, 1)

                        def x_lo(t):
                            dve.wait_ge(s_xhi, at(a, NT, t + 1))
                            cols = slice(t * P, (t + 1) * P)
                            low(xT[1][:, :, cols], xT2[64:P, cols], (ps_a, ps_b)[t], xT[0][:, :, cols], xT2[0:64, cols],
                                s_xlo, 0)

                        def q_lo(m):
                            dve.wait_ge(s_qhi, at(a, 3, m + 1))
                            ps = (ps_a, ps_b)[m % 2]
                            q = par(a)
                            if m < 2:
                                nc.vector.tensor_tensor(qT[q][1][:, m, :], ps[:, 0:S], qT[q][0][:, m, :].bitcast(fp32),
                                                        ALU.subtract).then_inc(s_qlo, 1)
                            else:
                                nc.vector.tensor_tensor(qT2[q][64:P, :], ps[64:P, 0:S], qT2[q][0:64, :].bitcast(fp32),
                                                        ALU.subtract).then_inc(s_qlo, 1)

                        def maxima(m):
                            h4, t = m // NT, m % NT
                            dve.wait_ge(s_mps, at(a, NT * QUADS, m + 1))
                            if m == 0:
                                dve.wait_ge(s_mk, at(a, 1, 1))
                            ps = ps_m[m % 2][:, 0:QUAD].rearrange("p (h k) -> p h k", k=KEYS)
                            nc.vector.tensor_tensor(ip_masked[m % 2][:], ps[:, :, T:KEYS],
                                                    stats[:, t:t + 1, R_MASK:R_MASK + NIP].broadcast_to([P, 4, NIP]),
                                                    ALU.add).then_inc(s_dve, 1)
                            nc.vector.tensor_reduce(stats[:, t, R_MT + 4 * h4:R_MT + 4 * h4 + 4], ps[:, :, 0:T], AX.X, ALU.max)
                            dve.wait_ge(s_dve, at(a, NT * QUADS, m + 1))
                            nc.vector.tensor_reduce(stats[:, t, R_MI + 4 * h4:R_MI + 4 * h4 + 4], ip_masked[m % 2][:],
                                                    AX.X, ALU.max).then_inc(s_mx, 1)

                        def norm(u):
                            g = u % 3
                            ns = 2 * GROUPS[g]
                            dve.wait_ge(s_pv, at(c, UNITS, u + 1))
                            o = ps_o[:, 0:ns * 17].rearrange("p (n c) -> p n c", c=17)
                            nc.vector.reciprocal(inv[:, 0:ns], o[:, :, 0]).then_inc(s_inv, 1)
                            wait(dve, s_at, c, UNITS, u - 1)
                            dve.wait_ge(s_inv, at(c, UNITS, u + 1))
                            nc.vector.tensor_tensor(heads[u % 2][:, 0:ns, :], o[:, :, 1:17],
                                                    inv[:, 0:ns].rearrange("p (n o) -> p n o", o=1).broadcast_to([P, ns, DH]),
                                                    ALU.mult).then_inc(s_nm, 1)

                        def a_lo(t):
                            dve.wait_ge(s_ahi, at(c, NT, t + 1))
                            cols = slice(t * P, (t + 1) * P)
                            low(aT[1][:, :, cols], aT2[64:P, cols], ps_b, aT[0][:, :, cols], aT2[0:64, cols], s_alo, 0)

                        def finish(t):
                            dve.wait_ge(s_op, at(c, NT, t + 1))
                            if t == 0:
                                dve.wait_ge(s_xb, at(c, 1, 1))
                                reg = c[0] is not None
                                if reg or c[1] >= 2:
                                    dve.wait_ge(s_y[par(c)], nth(c, 32, -32))
                            nc.vector.tensor_tensor(y[par(c)][:, t, :], ps_a[:, 0:D], x_bias[par(c)][:, t, :],
                                                    ALU.add).then_inc(s_yr, 1)

                        def spread_values():
                            dve.wait_ge(s_vals[par(b)], nth(b, 16 * NVDMA))
                            wait(dve, s_pv, b, UNITS, -UNITS)
                            v = values[par(b)][:].rearrange("p (t n c) -> p t n c", t=TILES, c=SLOT)
                            for t in range(0, TILES, 13):
                                nc.vector.tensor_tensor(
                                    v[:, :, :, 2:SLOT],
                                    raw_v[par(b)][:].rearrange("p t (o c) -> p t o c", o=1).broadcast_to([P, TILES, SLOTS, 3 * DH]),
                                    own_rows[:].rearrange("p t (n c) -> p t n c", n=SLOTS), ALU.mult).then_inc(s_vx, 1)

                        if A:
                            dve.wait_ge(s_keys[par(a)], nth(a, 16))
                            wait(dve, s_sc, b, PAIRS, 0)
                            spread_keys(nc.vector, a, 0)
                        if A:
                            wait(dve, s_et, a, 1, 0)
                            nc.vector.tensor_copy(stats[:, :, R_MASK:R_MASK + NIP],
                                                  mask[:, :, bass.ds(at(a, NIP, 0), NIP)]).then_inc(s_mk, 1)
                        for s in range(PAIRS):
                            if Bs and s == 2:
                                spread_values()
                            if A:
                                if s < 2:
                                    x_lo(s)
                                elif s < 5:
                                    q_lo(s - 2)
                                if s >= 3:
                                    for m in ([0], [1], [2, 3], [4, 5, 6])[s - 3]:
                                        maxima(m)
                            if Cs:
                                if s == 4:
                                    a_lo(0)
                                if s == 5:
                                    finish(0)
                                if s < UNITS:
                                    norm(s)
                                if s == 6:
                                    a_lo(1)
                        if A:
                            for m in (7, 8, 9):
                                maxima(m)
                        if Cs:
                            finish(1)

                    sched(dve, step)

                @block.gpsimd
                def _(pool):
                    def step(pool, b, n):
                        A, Bs, Cs = has(n)
                        a, c = off(b, 1), off(b, -1)
                        if A:
                            pool.wait_ge(s_keys[par(a)], nth(a, 16))
                            wait(pool, s_sc, b, PAIRS, 0)
                            spread_keys(nc.gpsimd, a, 1)
                        if Bs:
                            pool.wait_ge(s_x[par(b)], nth(b, 32))
                            wait(pool, s_yr, b, NT, -NT)
                            nc.gpsimd.tensor_tensor(x_bias[par(b)][:], x_in[par(b)][:, :, 0:D],
                                                    bias[:].rearrange("p (o d) -> p o d", o=1).broadcast_to([P, NT, D]),
                                                    ALU.add).then_inc(s_xb, 1)
                        for s in range(PAIRS):
                            if Bs:
                                pool.wait_ge(s_hi, at(b, PAIRS, s + 1))
                                w = S * (2 if 2 * s + 1 < TILES else 1)
                                nc.gpsimd.tensor_tensor(prob_lo[par(b)][:, s, 0:w], prob[:, s, 0:w],
                                                        prob_hi[par(b)][:, s, 0:w], ALU.subtract).then_inc(s_lo, 1)
                            if Cs and s < UNITS:
                                t, g = s // 3, s % 3
                                nh = GROUPS[g]
                                pool.wait_ge(s_nm, at(c, UNITS, s + 1))
                                wait(pool, s_att, c, NT, t + 1 - NT)
                                hv = heads[s % 2][:, 0:2 * nh, :].rearrange("p (h i) c -> p h i c", i=2)
                                for c0 in (GHEAD[g] * DH, D)[0:1 + g // 2]:
                                    last = nc.gpsimd.tensor_tensor(
                                        attn[:, t, c0:c0 + nh * DH].rearrange("p (h c) -> p h c", c=DH),
                                        hv[:, :, 0, :], hv[:, :, 1, :], ALU.add)
                                last.then_inc(s_at, 1)

                    sched(pool, step)


_INS = ["x", "ctx_2048", "fside_Bx4x4_0", "L0_xattn_w_q", "L0_xattn_w_k", "L0_xattn_w_v", "L0_xattn_w_k_ip",
        "L0_xattn_w_v_ip", "L0_xattn_w_out", "L0_xattn_b_out"]


def kernel(**inputs):
    import concourse.bacc as _bacc
    from concourse.bass_utils import run_bass_kernel_spmd as _run

    nc = _bacc.Bacc("TRN2", target_bir_lowering=False, num_devices=1)
    arrays, args = {}, []
    named = [(n, np.ascontiguousarray(inputs[n])) for n in _INS] + list(constants().items())
    for name, a in named:
        arrays[f"in_{name}_dram"] = a
        args.append(nc.dram_tensor(f"in_{name}_dram", a.shape, mybir.dt.from_np(a.dtype), kind="ExternalInput").ap())
    shape = tuple(inputs["x"].shape)
    args.append(nc.dram_tensor("out_0_dram", shape, fp32, kind="ExternalOutput").ap())
    xattn_kernel(nc, *args, shape[0])
    r = _run(nc, [arrays], core_ids=[0])
    return r.results[0]["out_0_dram"]
```

```python
import numpy as np
import concourse.bass as bass
from concourse import mybir
from contextlib import ExitStack

fp32 = mybir.dt.float32
f32r = mybir.dt.float32r
bf16 = mybir.dt.bfloat16
fp16 = mybir.dt.float16
ALU = mybir.AluOpType
ACT = mybir.ActivationFunctionType
AX = mybir.AxisListType

P = 128
B, S, D, C = 64, 256, 320, 512
H, DH = 20, 16
T, NIP = 69, 8
KEYS = T + NIP
NT = S // P
GW = 16
NEG = -10000.0
SHIFT = 5.0

GROUPS = [8, 8, 4]
GHEAD = [0, 8, 16]
GTILES = [-(-g * KEYS // P) for g in GROUPS]
GTILE = [sum(GTILES[:g]) for g in range(3)]
TILES = sum(GTILES)
ROWS = TILES * P
QUAD = 4 * KEYS
QUADS = H // 4
PAIRS = -(-TILES // 2)
RING = [0, 1, 2, 0, 1, 2, 1]
MAXIMA = [[], [], [0, 1, 2], [3, 4, 5], [6, 7], [8, 9], []]
UNITS = NT * 3
SLOT = 50
R_MT, R_MI, R_MASK, R_ONE = 0, H, 64, 80
KC = 4
CB = 4
CK = T + 1
DW = D + 64


def tile_parts():
    out = []
    for g, heads in enumerate(GROUPS):
        for t in range(GTILES[g]):
            r0, r1 = t * P, min((t + 1) * P, heads * KEYS)
            parts = []
            for h in range(r0 // KEYS, (r1 - 1) // KEYS + 1):
                k0, k1 = max(0, r0 - h * KEYS), min(KEYS, r1 - h * KEYS)
                for ip, (a, b) in enumerate(((k0, min(k1, T)), (max(k0, T), k1))):
                    if b > a:
                        parts.append((2 * h + ip, h * KEYS + a - r0, a, b - a))
            out.append((g, parts[0][0], parts))
    return out


PARTS = tile_parts()
NSLOTS = [p[-1][0] - s + 1 for _, s, p in PARTS]
SLOTS = max(NSLOTS)
VCOLS = TILES * SLOTS * SLOT
NVDMA = 6


def constants():
    sel = np.zeros((P, ROWS), np.float32)
    ones = np.zeros((P, VCOLS), np.float32)
    for t, (g, s0, parts) in enumerate(PARTS):
        for slot, row, key, n in parts:
            head = GHEAD[g] + slot // 2
            for r in range(n):
                col = t * P + row + r
                sel[(R_MI if slot % 2 else R_MT) + head, col] = -1.0
                if slot % 2:
                    sel[R_MASK + key + r - T, col] = 1.0
                sel[R_ONE, col] = 1.0
                c = (t * SLOTS + slot - s0) * SLOT + 1
                ones[row + r, c:c + SLOT - 1] = 1.0
    line = np.arange(GW, dtype=np.float32) * np.float32(1.0 / (GW - 1))
    grid = np.zeros((P, 4), np.float32)
    s = np.arange(P)
    grid[:, 0] = line[s % GW]
    grid[:, 1] = line[s // GW]
    grid[:, 2] = line[(s + P) // GW]
    own = np.zeros((P, 8 + 8 + 4), np.float32)
    for g, heads in enumerate(GROUPS):
        for h in range(heads):
            own[h * DH:(h + 1) * DH, GHEAD[g] + h] = 1.0
            if g == 2:
                own[64 + h * DH:64 + (h + 1) * DH, GHEAD[g] + h] = 1.0
    return {"c_sel": sel, "c_ones": ones, "c_grid": np.concatenate([grid, own], 1), "c_ident": np.eye(P, dtype=np.float32)}


def at(i, per, c):
    reg, off, step = i
    return per * off + c if reg is None else reg * (per * step) + (per * off + c)


def wait(eng, sem, i, per, c):
    v = at(i, per, c)
    if i[0] is not None or v > 0:
        eng.wait_ge(sem, v)


def xattn_kernel(nc, x, ctx, bbox, w_q, w_k, w_v, w_k_ip, w_v_ip, w_out, b_out,
                 c_sel, c_ones, c_grid, c_ident, out, NB):
    k_scratch = nc.dram_tensor("k_scratch", (NB, 3 * P, 2, KEYS), fp32, kind="Internal").ap()
    v_scratch = nc.dram_tensor("v_scratch", (NB, H, KEYS, 3 * DH), bf16, kind="Internal").ap()

    ctx_stack = ExitStack()
    with ctx_stack:
        def sb(name, shape, dt, stack=ctx_stack):
            return stack.enter_context(nc.sbuf_tensor(name, shape, dt))

        def sem(name):
            return ctx_stack.enter_context(nc.semaphore(name))

        ident = sb("ident", [P, P], fp32)
        grid = sb("grid", [P, 4 + H], fp32)
        own = grid[:, 4:4 + H]
        own_rows = sb("own_rows", [P, TILES, SLOTS * (SLOT - 2)], bf16)
        wq = [sb(f"wq_{n}", [P, 3, 384], f32r) for n in ("hi", "lo")]
        wo = [sb(f"wo_{n}", [P, 3, D], f32r) for n in ("hi", "lo")]
        sel = sb("sel", [P, ROWS], f32r)
        mask = sb("mask", [P, NT, NB * NIP], fp32)
        bias = sb("bias", [P, D], f32r)
        ones = sb("ones", [P, P], f32r)
        values = [sb(f"values{q}", [P, VCOLS], bf16) for q in range(2)]
        keys = [[sb(f"keys_{n}{q}", [P, ROWS], f32r) for n in ("hi", "lo")] for q in range(2)]
        raw_v = [sb(f"raw_v{q}", [P, TILES, 3 * DH], bf16) for q in range(2)]

        with ExitStack() as st:
            raw_q = sb("raw_q", [P, 3, 384], fp32, st)
            raw_o = sb("raw_o", [P, 3, D], fp32, st)
            raw_w = [sb(f"raw_w{n}", [P, KC, D], fp32, st) for n in range(4)]
            raw_c = sb("raw_c", [P, VCOLS], fp32, st)
            raw_b = sb("raw_b", [1, D], fp32, st)
            box = sb("box", [P, NB, 4, 4], fp32, st)
            inside = [sb(f"inside{n}", [P, NB, 4], fp32, st) for n in range(4)]
            anyin = sb("anyin", [P, NB], fp32, st)
            ctx_in = [sb(f"ctx_in{j}", [KEYS, C], fp32, st) for j in range(CB)]
            ctxT = [sb(f"ctxT_{n}", [P, KC, CB, CK], f32r, st) for n in ("hi", "lo")]
            ipT = [sb(f"ipT_{n}", [P, KC, CB * NIP], f32r, st) for n in ("hi", "lo")]
            w_hi = [sb(f"w_hi{n}", [P, KC, D], f32r, st) for n in range(4)]
            w_lo = [sb(f"w_lo{n}", [P, KC, D], f32r, st) for n in range(4)]
            k_stage = [sb(f"k_stage{m}", [P, 2, CB, KEYS], f32r, st) for m in range(3)]
            v_stage = [sb(f"v_stage{n}", [T, H, 3, DH], bf16, st) for n in range(5)]
            v_rest = [sb(f"v_rest{n}", [T, D], fp32, st) for n in range(5)]
            ps_t = [st.enter_context(nc.psum_tensor(f"ps_t{n}", [P, 512], fp32)) for n in range(2)]
            ps_k = [st.enter_context(nc.psum_tensor(f"ps_k{n}", [P, 512], fp32)) for n in range(3)]
            ps_v = [st.enter_context(nc.psum_tensor(f"ps_v{n}", [P, 512], fp32)) for n in range(3)]
            VBUF = [2, 0, 1, 0, 1]
            VROWS = [CB * NIP, T, T, T, T]

            s_const = sem("constants_loaded")
            s_w = sem("weights_loaded")
            s_w2 = sem("main_weights_loaded")
            s_ctx = [sem(f"context_loaded{j}") for j in range(CB)]
            s_setup = sem("setup_steps")
            s_zero = sem("zeroed")
            s_wsplit = sem("weights_split")
            s_t = sem("context_transposed")
            s_chi = sem("context_hi")
            s_clo = sem("context_lo")
            s_k = sem("keys_projected")
            s_khi = sem("keys_hi")
            s_klo = sem("keys_lo")
            s_v = sem("values_projected")
            s_vhi = sem("values_hi")
            s_vrest = sem("values_rest")
            s_vmid = sem("values_middle")
            s_vlo = sem("values_lo")
            s_kst = [sem(f"keys_stored{m}") for m in range(3)]
            s_vst = [sem(f"values_stored{n}") for n in range(5)]
            WN = (w_k, w_k_ip, w_v, w_v_ip)
            KW = [128, 128, 64]
            NI = NB // CB

            def steps(eng, body):
                body(eng, (None, -1, 1), False, True, NI > 1)
                body(eng, (None, 0, 1), True, NI > 1, NI > 2)
                if NI > 3:
                    with eng.Fori(1, NI - 2) as i:
                        body(eng, (i, 0, 1), True, True, True)
                for n in range(max(1, NI - 2), NI):
                    body(eng, (None, n, 1), True, n + 1 < NI, n + 2 < NI)

            with nc.Block() as block:

                @block.sync
                def _(sp):
                    sp.dma_start(ident[:], c_ident).then_inc(s_const, 16)
                    for n in range(4):
                        sp.dma_start(raw_w[n][:], WN[n].rearrange("(k p) n -> p k n", p=P)).then_inc(s_w, 16)

                    def load_context(i, j):
                        n = at(i, CB, j)
                        sp.dma_start(ctx_in[j][:], ctx[bass.ds(n, 1), :, :].rearrange("a k c -> (a k) c")
                                     ).then_inc(s_ctx[j], 16)

                    def store_values(i, u):
                        n = at(i, CB * H, (u - 1) * H)
                        sp.wait_ge(s_vlo, at(i, 5, u + 1))
                        if u > 0:
                            sp.dma_start(v_scratch.rearrange("b h k c -> (b h) k c")[bass.ds(n, H), 0:T, :].rearrange("h k c -> k h c"),
                                         v_stage[u][:].rearrange("k h s c -> k h (s c)")
                                         ).then_inc(s_vst[u], 16)
                            return
                        for j in range(CB):
                            sp.dma_start(v_scratch[bass.ds(at(i, CB, j), 1), :, T:KEYS, :].rearrange("a h k c -> (a k) h c"),
                                         v_stage[0][NIP * j:NIP * (j + 1)].rearrange("k h s c -> k h (s c)")
                                         ).then_inc(s_vst[0], 16)

                    def store_keys(i, m):
                        sp.wait_ge(s_klo, at(i, 3, m + 1))
                        n = at(i, CB, 0)
                        for h in range(2):
                            for r0 in (m * P, m * P + 64)[0:1 + m // 2]:
                                sp.dma_start(
                                    k_scratch[bass.ds(n, CB), r0:r0 + KW[m], h, :].rearrange("j p k -> p j k"),
                                    k_stage[m][0:KW[m], h].bitcast(fp32)).then_inc(s_kst[m], 16)

                    def body(sp, i, now, nxt, nxt2):
                        if not now:
                            for j in range(CB):
                                load_context((None, 0, 1), j)
                            for k in range(2):
                                sp.dma_start(raw_q[:, k, 0:D], w_q[k * P:(k + 1) * P, :]).then_inc(s_w2, 16)
                                sp.dma_start(raw_q[:, k, D:384], w_q[k * P:(k + 1) * P, 256:D]).then_inc(s_w2, 16)
                                sp.dma_start(raw_q[64 * k:64 * k + 64, 2, 0:D], w_q[256:D, :]).then_inc(s_w2, 16)
                                sp.dma_start(raw_q[64 * k:64 * k + 64, 2, D:384], w_q[256:D, 256:D]).then_inc(s_w2, 16)
                                sp.dma_start(raw_o[:, k, :], w_out[k * P:(k + 1) * P, :]).then_inc(s_w2, 16)
                                sp.dma_start(raw_o[64 * k:64 * k + 64, 2, :], w_out[256:D, :]).then_inc(s_w2, 16)
                            sp.dma_start(grid[:], c_grid).then_inc(s_w2, 16)
                            sp.dma_start(box[:].rearrange("p b m c -> p (b m c)"),
                                         bbox.rearrange("b m c -> (b m c)").partition_broadcast(P)).then_inc(s_w2, 16)
                            sp.dma_start(raw_b[:], b_out.rearrange("(o d) -> o d", o=1)).then_inc(s_w2, 16)
                            sp.dma_start(raw_c[:, 0:VCOLS], c_ones).then_inc(s_w2, 16)
                        for m in range(3):
                            if now:
                                store_keys(i, m)
                        if not nxt:
                            sp.wait_ge(s_wsplit, 8)
                            sp.wait_ge(s_setup, 4 + 6)
                            sp.dma_start(raw_c[:, 0:ROWS], c_sel).then_inc(s_const, 16)
                        for u in range(5):
                            if now:
                                store_values(i, u)
                            if nxt2 and u > 0:
                                sp.wait_ge(s_t, at(i, CB, CB + u))
                                load_context((i[0], i[1] + 2, i[2]), u - 1)

                    steps(sp, body)
                    for m in range(3):
                        sp.wait_ge(s_kst[m], (32 if m < 2 else 64) * NI)
                    for u in range(5):
                        sp.wait_ge(s_vst[u], (16 if u else 64) * NI)

                @block.tensor
                def _(pe):
                    pe.wait_ge(s_const, 16)

                    def three(ps, stat, mov, skip=False, first=True):
                        for k in range(KC):
                            for n, (a, b) in enumerate(((0, 0), (0, 1), (1, 0))):
                                last = nc.tensor.matmul(ps, stat(a, k), mov(b, k), start=first and k == 0 and n == 0,
                                                        stop=k == KC - 1 and n == 2, skip_group_check=skip)
                        return last

                    def transposes(i, j):
                        pe.wait_ge(s_ctx[j], at(i, 16, 16))
                        wait(pe, s_clo, i, CB, j - 1)
                        for k in range(KC):
                            last = nc.tensor.transpose(ps_t[j % 2][:, k * KEYS:(k + 1) * KEYS],
                                                       ctx_in[j][:, k * P:(k + 1) * P], ident[0:KEYS, 0:KEYS])
                        last.then_inc(s_t, 1)

                    def project_keys(i, m):
                        if m == 0:
                            pe.wait_ge(s_clo, at(i, CB, CB))
                        wait(pe, s_klo, i, 3, m - 2)
                        cols = slice(m * P, m * P + KW[m])
                        three(ps_k[m][0:KW[m], 0:CB * CK], lambda a, k: (w_hi, w_lo)[a][0][:, k, cols],
                              lambda b, k: ctxT[b][:, k].rearrange("p j k -> p (j k)"), skip=True)
                        last = three(ps_k[m][0:KW[m], CB * CK:CB * CK + CB * NIP],
                                     lambda a, k: (w_hi, w_lo)[a][1][:, k, cols],
                                     lambda b, k: ipT[b][:, k, :], skip=True, first=False)
                        last.then_inc(s_k, 1)

                    def project_values(i, u):
                        wait(pe, s_vrest, i, 5, [-4, -1, 0, 2, 3][u])
                        n, r = VBUF[u], VROWS[u]
                        three(ps_v[n][0:r, 0:D],
                              (lambda a, k: ipT[a][:, k, :]) if u == 0 else (lambda a, k: ctxT[a][:, k, u - 1, 0:T]),
                              lambda b, k: (w_hi, w_lo)[b][3 if u == 0 else 2][:, k, :]).then_inc(s_v, 1)

                    def body(pe, i, now, nxt, nxt2):
                        ni = (i[0], i[1] + 1, i[2])
                        if now:
                            if i[0] is None and i[1] == 0:
                                pe.wait_ge(s_wsplit, 2)
                            for m in range(3):
                                project_keys(i, m)
                            if i[0] is None and i[1] == 0:
                                pe.wait_ge(s_wsplit, 4)
                        for u in range(5):
                            if now:
                                project_values(i, u)
                            if nxt and u > 0:
                                transposes(ni, u - 1)

                    steps(pe, body)

                @block.scalar
                def _(act):
                    act.wait_ge(s_zero, 1)

                    def v_hi(i, u):
                        act.wait_ge(s_v, at(i, 5, u + 1))
                        wait(act, s_vst[u], i, 16 if u else 64, 0)
                        n, r = VBUF[u], VROWS[u]
                        nc.scalar.copy(v_stage[u][0:r, :, 0, :],
                                       ps_v[n][0:r, 0:D].rearrange("p (h c) -> p h c", c=DH)).then_inc(s_vhi, 1)

                    def v_mid(i, u):
                        act.wait_ge(s_vrest, at(i, 5, u + 1))
                        r = VROWS[u]
                        nc.scalar.copy(v_stage[u][0:r, :, 1, :],
                                       v_rest[u][0:r, :].rearrange("p (h c) -> p h c", c=DH)).then_inc(s_vmid, 1)

                    def k_hi(i, m):
                        act.wait_ge(s_k, at(i, 3, m + 1))
                        wait(act, s_kst[m], i, 32 if m < 2 else 64, 0)
                        w = KW[m]
                        nc.scalar.mul(k_stage[m][0:w, 0, :, 0:T],
                                      ps_k[m][0:w, 0:CB * CK].rearrange("p (j k) -> p j k", j=CB)[:, :, 0:T], 0.25)
                        nc.scalar.mul(k_stage[m][0:w, 0, :, T:KEYS],
                                      ps_k[m][0:w, CB * CK:CB * (CK + NIP)].rearrange("p (j k) -> p j k", j=CB),
                                      0.25).then_inc(s_khi, 1)

                    def context_hi(i, j):
                        act.wait_ge(s_t, at(i, CB, j + 1))
                        ps = ps_t[j % 2][:, 0:KC * KEYS].rearrange("p (k n) -> p k n", k=KC)
                        nc.scalar.copy(ctxT[0][:, :, j, 0:T], ps[:, :, 0:T])
                        nc.scalar.copy(ipT[0][:, :, NIP * j:NIP * (j + 1)], ps[:, :, T:KEYS]).then_inc(s_chi, 1)

                    def body(act, i, now, nxt, nxt2):
                        for m in range(3):
                            if now:
                                k_hi(i, m)
                        for u in range(5):
                            if now:
                                v_hi(i, u)
                                if u > 0:
                                    v_mid(i, u - 1)
                            if nxt and u > 0:
                                context_hi((i[0], i[1] + 1, i[2]), u - 1)
                        if now:
                            v_mid(i, 4)

                    steps(act, body)

                @block.vector
                def _(dve):
                    n_setup = [0]

                    def then(ins):
                        n_setup[0] += 1
                        ins.then_inc(s_setup, 1)
                        dve.wait_ge(s_setup, n_setup[0])

                    for a in ctxT:
                        last = nc.vector.memset(a[:].bitcast(fp32), 0.0)
                    last.then_inc(s_zero, 1)
                    dve.wait_ge(s_w, 16 * 4)
                    def split_weights(n):
                        then(nc.vector.tensor_copy(w_hi[n][:], raw_w[n][:]))
                        nc.vector.tensor_tensor(w_lo[n][:], raw_w[n][:], w_hi[n][:].bitcast(fp32),
                                                ALU.subtract).then_inc(s_wsplit, 1)

                    def context_lo(i, j):
                        dve.wait_ge(s_chi, at(i, CB, j + 1))
                        ps = ps_t[j % 2][:, 0:KC * KEYS].rearrange("p (k n) -> p k n", k=KC)
                        ip = slice(NIP * j, NIP * (j + 1))
                        nc.vector.tensor_tensor(ctxT[1][:, :, j, 0:T], ps[:, :, 0:T],
                                                ctxT[0][:, :, j, 0:T].bitcast(fp32), ALU.subtract)
                        nc.vector.tensor_tensor(ipT[1][:, :, ip], ps[:, :, T:KEYS],
                                                ipT[0][:, :, ip].bitcast(fp32), ALU.subtract).then_inc(s_clo, 1)

                    def k_lo(i, m):
                        dve.wait_ge(s_khi, at(i, 3, m + 1))
                        w = KW[m]
                        nc.vector.scalar_tensor_tensor(
                            out=k_stage[m][0:w, 1, :, 0:T],
                            in0=ps_k[m][0:w, 0:CB * CK].rearrange("p (j k) -> p j k", j=CB)[:, :, 0:T],
                            scalar=0.25, in1=k_stage[m][0:w, 0, :, 0:T].bitcast(fp32),
                            op0=ALU.mult, op1=ALU.subtract)
                        nc.vector.scalar_tensor_tensor(
                            out=k_stage[m][0:w, 1, :, T:KEYS],
                            in0=ps_k[m][0:w, CB * CK:CB * (CK + NIP)].rearrange("p (j k) -> p j k", j=CB),
                            scalar=0.25, in1=k_stage[m][0:w, 0, :, T:KEYS].bitcast(fp32),
                            op0=ALU.mult, op1=ALU.subtract).then_inc(s_klo, 1)

                    def v_left(i, u):
                        dve.wait_ge(s_vhi, at(i, 5, u + 1))
                        n, r = VBUF[u], VROWS[u]
                        nc.vector.tensor_tensor(v_rest[u][0:r, :].rearrange("p (h c) -> p h c", c=DH),
                                                ps_v[n][0:r, 0:D].rearrange("p (h c) -> p h c", c=DH),
                                                v_stage[u][0:r, :, 0, :], ALU.subtract).then_inc(s_vrest, 1)

                    def ones_of_values():
                        dve.wait_ge(s_w2, 16 * (12 + 4))
                        for q in range(2):
                            nc.vector.tensor_copy(values[q][:], raw_c[:, 0:VCOLS]).then_inc(s_wsplit, 1)

                    def split_main(a, raw):
                        then(nc.vector.tensor_copy(a[0][:], raw[:]))
                        nc.vector.tensor_tensor(a[1][:], raw[:], a[0][:].bitcast(fp32), ALU.subtract).then_inc(s_wsplit, 1)

                    def split_bias():
                        nc.vector.memset(ones[:].bitcast(fp32), 1.0)
                        then(nc.vector.memset(bias[:].bitcast(fp32), 0.0))
                        then(nc.vector.tensor_copy(bias[0:1, :], raw_b[:]))
                        then(nc.vector.tensor_tensor(bias[32:33, :], raw_b[:], bias[0:1, :].bitcast(fp32), ALU.subtract))

                    def make_own_rows():
                        then(nc.vector.tensor_copy(
                            own_rows[:].rearrange("p t (n c) -> p (t n) c", n=SLOTS),
                            raw_c[:, 0:VCOLS].rearrange("p (n c) -> p n c", c=SLOT)[:, :, 2:SLOT]))

                    def make_mask(t):
                        xg, yg = grid[:, 0:1], grid[:, 1 + t:2 + t]
                        then(nc.vector.tensor_scalar(inside[0][:], box[:, :, :, 0], xg, None, ALU.is_le))
                        for n, c, g, op in ((1, 2, xg, ALU.is_ge), (2, 1, yg, ALU.is_le), (3, 3, yg, ALU.is_ge)):
                            then(nc.vector.scalar_tensor_tensor(out=inside[n][:], in0=box[:, :, :, c], scalar=g,
                                                                in1=inside[n - 1][:], op0=op, op1=ALU.mult))
                        then(nc.vector.tensor_reduce(anyin[:], inside[3][:], AX.X, ALU.max))
                        mt = mask[:, t, :].rearrange("p (b k) -> p b k", k=NIP)
                        nc.vector.tensor_scalar(mt[:, :, 4:8], inside[3][:], -NEG, NEG, ALU.mult, ALU.add)
                        then(nc.vector.tensor_scalar(mt[:, :, 0:4], anyin[:].rearrange("p (b o) -> p b o", o=1).broadcast_to([P, NB, 4]),
                                                     NEG, None, ALU.mult))

                    def body(dve, i, now, nxt, nxt2):
                        before_last, last = not nxt2 and nxt and now, not nxt
                        if not now:
                            for n in (0, 1):
                                split_weights(n)
                        if before_last:
                            ones_of_values()
                        if last:
                            make_own_rows()
                        for m in range(3):
                            if now:
                                k_lo(i, m)
                            if before_last and m == 1:
                                split_bias()
                            elif before_last:
                                split_main(*((wq, raw_q), None, (wo, raw_o))[m])
                            if last and m < NT:
                                make_mask(m)
                        for u in range(5):
                            if now:
                                v_left(i, u)
                            if nxt and u > 0:
                                context_lo((i[0], i[1] + 1, i[2]), u - 1)
                        if not now:
                            for n in (3, 2):
                                split_weights(n)

                    steps(dve, body)

                    dve.wait_ge(s_const, 32)
                    then(nc.vector.tensor_copy(sel[:], raw_c[:, 0:ROWS]))

                @block.gpsimd
                def _(pool):
                    for q in range(2):
                        for a in keys[q]:
                            nc.gpsimd.memset(a[:].bitcast(fp32), 0.0)
                        nc.gpsimd.memset(raw_v[q][:], 0.0)

                    def body(pool, i, now, nxt, nxt2):
                        for u in range(5 if now else 0):
                            pool.wait_ge(s_vmid, at(i, 5, u + 1))
                            r = VROWS[u]
                            nc.gpsimd.tensor_tensor(v_stage[u][0:r, :, 2, :],
                                                    v_rest[u][0:r, :].rearrange("p (h c) -> p h c", c=DH),
                                                    v_stage[u][0:r, :, 1, :], ALU.subtract).then_inc(s_vlo, 1)
                    steps(pool, body)

        with ExitStack() as st:
            raw_k = [sb(f"raw_k{q}", [P, 3, 2, KEYS], fp32, st) for q in range(2)]
            x_in = [sb(f"x_in{q}", [P, NT, DW], fp32, st) for q in range(2)]
            x_keep = [sb(f"x_keep{q}", [P, NT, D], fp32, st) for q in range(2)]
            y = [sb(f"y{q}", [P, NT, D], fp32, st) for q in range(2)]
            xT = [sb(f"xT_{n}", [P, 2, S], f32r, st) for n in ("hi", "lo")]
            xT2 = sb("xT2", [P, S], f32r, st)
            qT = [[sb(f"qT_{n}{q}", [P, 2, S], f32r, st) for n in ("hi", "lo")] for q in range(2)]
            qT2 = [sb(f"qT2_{q}", [P, S], f32r, st) for q in range(2)]
            stats = sb("stats", [P, NT, P], fp32, st)
            extra = sb("extra", [P, S], f32r, st)
            ip_masked = [sb(f"ip_masked{n}", [P, 4, NIP], fp32, st) for n in range(2)]
            prob = sb("prob", [P, PAIRS, 2 * S], fp32, st)
            prob_hi = [sb(f"prob_hi{q}", [P, PAIRS, 2 * S], fp16, st) for q in range(2)]
            prob_lo = [sb(f"prob_lo{q}", [P, PAIRS, 2 * S], fp16, st) for q in range(2)]
            inv = sb("inv", [P, 16], fp32, st)
            heads = [sb(f"heads{n}", [P, 16, DH], fp32, st) for n in range(2)]
            attn = sb("attn", [P, NT, DW], fp32, st)
            aT = [sb(f"aT_{n}", [P, 2, S], f32r, st) for n in ("hi", "lo")]
            aT2 = sb("aT2", [P, S], f32r, st)
            ps_s = [st.enter_context(nc.psum_tensor(f"ps_s{n}", [P, 512], fp32)) for n in range(3)]
            ps_m = [st.enter_context(nc.psum_tensor(f"ps_m{n}", [P, 512], fp32)) for n in range(2)]
            ps_o = st.enter_context(nc.psum_tensor("ps_o", [P, 512], fp32))
            ps_a = st.enter_context(nc.psum_tensor("ps_a", [P, 512], fp32))
            ps_b = st.enter_context(nc.psum_tensor("ps_b", [P, 512], fp32))

            s_x = [sem(f"x_loaded{q}") for q in range(2)]
            s_keys = [sem(f"keys_loaded{q}") for q in range(2)]
            s_vals = [sem(f"values_loaded{q}") for q in range(2)]
            s_kx = [sem(f"keys_{n}_spread") for n in ("hi", "lo")]
            s_vx = sem("values_spread")
            s_y = [sem(f"y_stored{q}") for q in range(2)]
            s_xt = sem("x_transposed")
            s_xhi = sem("xT_hi_ready")
            s_xlo = sem("xT_ready")
            s_q = sem("q_projected")
            s_qhi = sem("qT_hi_ready")
            s_qlo = sem("qT_ready")
            s_mps = sem("max_scores")
            s_mx = sem("max_found")
            s_dve = sem("masked_ip_ready")
            s_mk = sem("mask_in_stats")
            s_et = sem("stats_transposed")
            s_ex = sem("extra_ready")
            s_sc = sem("scores_ready")
            s_hi = sem("probs_hi_ready")
            s_lo = sem("probs_lo_ready")
            s_pv = sem("heads_summed")
            s_inv = sem("inverse_ready")
            s_nm = sem("heads_normed")
            s_at = sem("attn_ready")
            s_att = sem("attn_transposed")
            s_ahi = sem("aT_hi_ready")
            s_alo = sem("aT_ready")
            s_op = sem("out_projected")
            s_yr = sem("y_ready")
            s_xk = sem("x_kept")
            s_z = sem("stats_zeroed")

            def sched(eng, step):
                first, last = min(4, NB), max(NB - 2, min(4, NB))
                last -= (last - first) % 2
                for b in range(-1, first):
                    step(eng, (None, b, 1), b)
                if last > first:
                    with eng.Fori(0, (last - first) // 2) as i:
                        for o in range(2):
                            step(eng, (i, first + o, 2), None)
                for b in range(last, NB + 2):
                    step(eng, (None, b, 1), b)

            def par(b):
                return b[1] % 2

            def nth(b, per, c=0):
                reg, off, stp = b
                return per * (off // 2 + 1) + c if reg is None else reg * (per * stp // 2) + (per * (off // 2 + 1) + c)

            def off(b, n):
                return (b[0], b[1] + n, b[2])

            def has(n):
                return (True,) * 4 if n is None else tuple(0 <= n + o < NB for o in (1, 0, -1, -2))

            def quad_cols(h4):
                g = h4 // 2 if h4 < 4 else 2
                c = GTILE[g] * P + (h4 % 2 if h4 < 4 else 0) * QUAD
                return g, slice(c, c + QUAD)

            def spread_keys(eng, b, half, g):
                c, heads = GTILE[g] * P, GROUPS[g]
                eng.tensor_tensor(
                    keys[par(b)][half][:, c:c + heads * KEYS].rearrange("p (h k) -> p h k", k=KEYS),
                    raw_k[par(b)][:, g, half:half + 1, :].broadcast_to([P, heads, KEYS]),
                    own[:, GHEAD[g]:GHEAD[g] + heads].rearrange("p (h o) -> p h o", o=1).broadcast_to([P, heads, KEYS]),
                    ALU.mult).then_inc(s_kx[half], 1)

            with nc.Block() as block:

                @block.sync
                def _(sp):
                    def load_x(b):
                        xb = x[bass.ds(at(b, 1, 0), 1), :, :].rearrange("a (t p) d -> (a p) t d", p=P)
                        sp.dma_start(x_in[par(b)][:, :, 0:D], xb).then_inc(s_x[par(b)], 16)
                        sp.dma_start(x_in[par(b)][:, :, D:DW], xb[:, :, 256:D]).then_inc(s_x[par(b)], 16)

                    def load_keys(b):
                        sp.dma_start(raw_k[par(b)][:], k_scratch[bass.ds(at(b, 1, 0), 1), :, :, :]
                                     .rearrange("a (g p) s k -> (a p) g s k", p=P)).then_inc(s_keys[par(b)], 16)

                    def load_values(b):
                        for g, heads in enumerate(GROUPS):
                            src = v_scratch[bass.ds(at(b, 1, 0), 1), GHEAD[g]:GHEAD[g] + heads, :, :].rearrange("a h k c -> (a h k) c")
                            full, rest = GTILES[g] - 1, heads * KEYS - (GTILES[g] - 1) * P
                            sp.dma_start(raw_v[par(b)][:, GTILE[g]:GTILE[g] + full, :],
                                         src[0:full * P, :].rearrange("(t p) c -> p t c", p=P)).then_inc(s_vals[par(b)], 16)
                            sp.dma_start(raw_v[par(b)][0:rest, GTILE[g] + full, :],
                                         src[full * P:full * P + rest, :]).then_inc(s_vals[par(b)], 16)

                    def step(sp, b, n):
                        A, Bs, Cs, Ds = has(n)
                        if n == -1:
                            for b in range(min(2, NB)):
                                load_x((None, b, 1))
                                load_keys((None, b, 1))
                                load_values((None, b, 1))
                            return
                        def store(c, t):
                            sp.wait_ge(s_yr, at(c, NT, t + 1))
                            sp.dma_start(out[bass.ds(at(c, 1, 0), 1), t * P:(t + 1) * P, :].rearrange("a p d -> (a p) d"),
                                         y[par(c)][:, t, :]).then_inc(s_y[par(c)], 16)

                        if Ds:
                            store(off(b, -2), 1)
                        if n is None or n + 2 < NB:
                            sp.wait_ge(s_xk, at(b, NT, NT))
                            sp.wait_ge(s_xt, at(b, NT, NT))
                            load_x(off(b, 2))
                            for m in range(2):
                                sp.wait_ge(s_kx[m], at(b, 3, 3))
                            load_keys(off(b, 2))
                            sp.wait_ge(s_vx, at(b, 3, 3))
                            load_values(off(b, 2))
                        if Cs:
                            store(off(b, -1), 0)

                    sched(sp, step)
                    for q in range(2):
                        if NB > q:
                            sp.wait_ge(s_y[q], 32 * ((NB - q + 1) // 2))

                @block.tensor
                def _(pe):
                    mm = nc.tensor.matmul

                    def x_transpose(b, t, n):
                        if t == 0:
                            pe.wait_ge(s_x[par(b)], nth(b, 32))
                            if n is None or n >= 2:
                                pe.wait_ge(s_yr, at(b, NT, 1 - 3 * NT))
                            elif n >= 0:
                                pe.wait_ge(s_qlo, at(b, 3, 0))
                        else:
                            wait(pe, s_ex, b, 1, 0)
                        ps = (ps_a, ps_b)[t]
                        for k in range(2):
                            nc.tensor.transpose(ps[:, k * P:(k + 1) * P], x_in[par(b)][:, t, k * P:(k + 1) * P], ident[:])
                        nc.tensor.transpose(ps[:, 2 * P:3 * P], x_in[par(b)][:, t, 256:DW], ident[:]).then_inc(s_xt, 1)

                    def split_product(ps, hi, lo, both, w, cols, swap, first=True):
                        terms = []
                        for k in range(2):
                            terms += [(hi(k), w[0][:, k, cols]), (hi(k), w[1][:, k, cols]), (lo(k), w[0][:, k, cols])]
                        terms += [(both, w[0][:, 2, cols]), (both, w[1][:, 2, cols])]
                        for n, (a, ww) in enumerate(terms):
                            last = mm(ps, ww if swap else a, a if swap else ww, start=first and n == 0, stop=n == len(terms) - 1)
                        return last

                    def project(b, m):
                        if m == 0:
                            pe.wait_ge(s_xlo, at(b, NT, NT))
                        if m == 1:
                            pe.wait_ge(s_qlo, at(b, 3, 1))
                        if m == 2:
                            wait(pe, s_yr, b, NT, -2 * NT)
                        ps = (ps_b, ps_b, ps_a)[m]
                        split_product(ps[:, 0:S], lambda k: xT[0][:, k, :], lambda k: xT[1][:, k, :], xT2[:, :],
                                      wq, slice(m * P, (m + 1) * P), True).then_inc(s_q, 1)

                    def max_scores(b, n):
                        h4, t = n // NT, n % NT
                        g, cols = quad_cols(h4)
                        pe.wait_ge(s_qlo, at(b, 3, g + 1)) if n % 4 == 0 else None
                        if n == 0:
                            pe.wait_ge(s_kx[0], at(b, 3, 3))
                        wait(pe, s_mx, b, NT * QUADS, n - 1)
                        stat = qT[par(b)][0][:, g, t * P:(t + 1) * P] if g < 2 else qT2[par(b)][:, t * P:(t + 1) * P]
                        mm(ps_m[n % 2][:, 0:QUAD], stat, keys[par(b)][0][:, cols], start=True, stop=True).then_inc(s_mps, 1)

                    def stats_transpose(b, n):
                        pe.wait_ge(s_mx, at(b, NT * QUADS, NT * QUADS))
                        if n is None or n >= 1:
                            pe.wait_ge(s_alo, at(b, NT, 1 - 2 * NT))
                        else:
                            pe.wait_ge(s_qlo, at(b, 3, 2))
                        for t in range(NT):
                            last = nc.tensor.transpose(ps_b[:, t * P:(t + 1) * P], stats[:, t, :], ident[:])
                        last.then_inc(s_et, 1)

                    def scores(b, s):
                        wait(pe, s_hi, b, PAIRS, [-3, 0, -1, 1, 2, 3, 5][s])
                        if s == 0:
                            pe.wait_ge(s_kx[1], at(b, 3, 3))
                        q = par(b)
                        for o, t in enumerate(range(2 * s, min(2 * s + 2, TILES))):
                            ps = ps_s[RING[s]][:, o * S:(o + 1) * S]
                            g = PARTS[t][0]
                            c = slice(t * P, (t + 1) * P)
                            if g < 2:
                                mm(ps, keys[q][0][:, c], qT[q][0][:, g, :], start=True, stop=False)
                                mm(ps, keys[q][0][:, c], qT[q][1][:, g, :], start=False, stop=False)
                                mm(ps, keys[q][1][:, c], qT[q][0][:, g, :], start=False, stop=False)
                            else:
                                mm(ps, keys[q][0][:, c], qT2[q][:, :], start=True, stop=False)
                                mm(ps, keys[q][1][:, c], qT2[q][:, :], start=False, stop=False)
                            if t == 0:
                                pe.wait_ge(s_ex, at(b, 1, 1))
                            last = mm(ps, sel[:, c], extra[:, :], start=False, stop=True)
                        last.then_inc(s_sc, 1)

                    def sum_heads(b, u):
                        t, g = u // 3, u % 3
                        q = par(b)
                        if u == 0:
                            pe.wait_ge(s_vx, at(b, 3, 3))
                        if t == 0:
                            pe.wait_ge(s_lo, at(b, PAIRS, (3, 5, 7)[g]))
                        wait(pe, s_nm, b, UNITS, u)
                        first = True
                        for tt in range(GTILE[g], GTILE[g] + GTILES[g]):
                            s0, ns = PARTS[tt][1], NSLOTS[tt]
                            c = (tt % 2) * S + t * P
                            v = values[q][:, tt * SLOTS * SLOT:(tt * SLOTS + ns) * SLOT].rearrange("p (n c) -> p n c", c=SLOT)
                            o = ps_o[:, s0 * 17:(s0 + ns) * 17].rearrange("p (n c) -> p n c", c=17)
                            for pr, parts in ((prob_hi, 3), (prob_lo, 2)):
                                stat = pr[q][:, tt // 2, c:c + P]
                                for part in range(parts):
                                    a, w, oo = (1, 17, 0) if part == 0 else (2 + 16 * part, 16, 1)
                                    last = mm(o[:, :, oo:oo + w], stat, v[:, :, a:a + w], start=first, stop=False,
                                              skip_group_check=True)
                                    first = False
                        last.then_inc(s_pv, 1)

                    def attn_transpose(b, t, A, n):
                        pe.wait_ge(s_at, at(b, UNITS, 3 * t + 3))
                        ps = (ps_b, ps_a)[t]
                        if t == 1 and A:
                            pe.wait_ge(s_xlo, at(b, NT, 3 * NT + 1))
                        elif t == 1:
                            pe.wait_ge(s_yr, at(b, NT, 1))
                        elif A:
                            pe.wait_ge(s_qlo, at(b, 3, 3 * 2 + 2))
                        elif n == NB - 1:
                            pe.wait_ge(s_ex, NB)
                        else:
                            wait(pe, s_alo, b, NT, 1 - NT)
                        for k in range(2):
                            nc.tensor.transpose(ps[:, k * P:(k + 1) * P], attn[:, t, k * P:(k + 1) * P], ident[:])
                        nc.tensor.transpose(ps[:, 2 * P:3 * P], attn[:, t, 256:DW], ident[:]).then_inc(s_att, 1)

                    def project_out(b, t, A):
                        pe.wait_ge(s_alo, at(b, NT, t + 1))
                        if t == 0 and A:
                            pe.wait_ge(s_qlo, at(b, 3, 3 * 2 + 3))
                        elif t == 0:
                            wait(pe, s_yr, b, NT, 0)
                        c = slice(t * P, (t + 1) * P)
                        mm(ps_a[:, 0:D], ones[:], bias[:], start=True, stop=False)
                        split_product(ps_a[:, 0:D], lambda k: aT[0][:, k, c], lambda k: aT[1][:, k, c], aT2[:, c],
                                      wo, slice(0, D), False, False).then_inc(s_op, 1)

                    def step(pe, b, n):
                        A, Bs, Cs, Ds = has(n)
                        a, c = off(b, 1), off(b, -1)
                        d = off(b, -2)
                        for s in range(PAIRS):
                            if A and s == 0:
                                x_transpose(a, 0, n)
                            if Bs:
                                scores(b, s)
                            if A and s == 0:
                                x_transpose(a, 1, n)
                            if Ds and s == 1:
                                attn_transpose(d, 1, A, n)
                            if Ds and s == 2:
                                project_out(d, 1, A)
                            if A and s in (1, 2, 3):
                                project(a, s - 1)
                            if A and MAXIMA[s]:
                                max_scores(a, MAXIMA[s][0])
                            if Cs:
                                if s == 4:
                                    attn_transpose(c, 0, A, n)
                                if s == 5:
                                    project_out(c, 0, A)
                                if s < UNITS:
                                    sum_heads(c, s)
                            if A:
                                for m in MAXIMA[s][1:]:
                                    max_scores(a, m)
                        if A:
                            stats_transpose(a, n)

                    sched(pe, step)

                @block.scalar
                def _(act):
                    def step(act, b, n):
                        A, Bs, Cs, Ds = has(n)
                        a, c = off(b, 1), off(b, -1)

                        def x_hi(t):
                            act.wait_ge(s_xt, at(a, NT, t + 1))
                            ps = (ps_a, ps_b)[t]
                            cols = slice(t * P, (t + 1) * P)
                            nc.scalar.copy(xT[0][:, :, cols], ps[:, 0:2 * P].rearrange("p (k s) -> p k s", k=2))
                            nc.scalar.copy(xT2[0:64, cols], ps[0:64, 2 * P:3 * P]).then_inc(s_xhi, 1)

                        def q_hi(m):
                            act.wait_ge(s_q, at(a, 3, m + 1))
                            ps = (ps_b, ps_b, ps_a)[m]
                            if m < 2:
                                nc.scalar.copy(qT[par(a)][0][:, m, :], ps[:, 0:S]).then_inc(s_qhi, 1)
                            else:
                                nc.scalar.copy(qT2[par(a)][0:64, :], ps[0:64, 0:S]).then_inc(s_qhi, 1)

                        def a_hi(c, t):
                            act.wait_ge(s_att, at(c, NT, t + 1))
                            ps = (ps_b, ps_a)[t]
                            cols = slice(t * P, (t + 1) * P)
                            nc.scalar.copy(aT[0][:, :, cols], ps[:, 0:2 * P].rearrange("p (k s) -> p k s", k=2))
                            nc.scalar.copy(aT2[0:64, cols], ps[0:64, 2 * P:3 * P]).then_inc(s_ahi, 1)

                        for s in range(PAIRS):
                            if A and s == 0:
                                x_hi(0)
                            if Bs:
                                act.wait_ge(s_sc, at(b, PAIRS, s + 1))
                                wait(act, s_lo, b, PAIRS, s + 1 - PAIRS)
                                w = S * (2 if 2 * s + 1 < TILES else 1)
                                nc.scalar.activation(prob[:, s, 0:w], ps_s[RING[s]][:, 0:w], ACT.Exp)
                                nc.scalar.activation(prob_hi[par(b)][:, s, 0:w], ps_s[RING[s]][:, 0:w], ACT.Exp
                                                     ).then_inc(s_hi, 1)
                            if A:
                                if s == 0:
                                    x_hi(1)
                            if Ds and s == 1:
                                a_hi(off(b, -2), 1)
                            if A and s in (1, 2, 3):
                                q_hi(s - 1)
                            if Bs and s == 3:
                                act.wait_ge(s_x[par(b)], nth(b, 32))
                                wait(act, s_yr, b, NT, -NT)
                                nc.scalar.copy(x_keep[par(b)][:], x_in[par(b)][:, :, 0:D]).then_inc(s_xk, NT)
                            if Cs and s == 4:
                                a_hi(c, 0)
                        if A:
                            act.wait_ge(s_et, at(a, 1, 1))
                            nc.scalar.copy(extra[:, :], ps_b[:, 0:S]).then_inc(s_ex, 1)

                    sched(act, step)

                @block.vector
                def _(dve):
                    nc.vector.memset(stats[:], 0.0).then_inc(s_z, 1)
                    dve.wait_ge(s_z, 1)
                    nc.vector.memset(stats[:, :, R_ONE:R_ONE + 1], SHIFT).then_inc(s_z, 1)
                    dve.wait_ge(s_z, 2)

                    def step(dve, b, n):
                        A, Bs, Cs, Ds = has(n)
                        a, c = off(b, 1), off(b, -1)

                        def low(dst, dst2, ps, hi, hi2, sem_, w):
                            nc.vector.tensor_tensor(dst, ps[:, 0:2 * P].rearrange("p (k s) -> p k s", k=2),
                                                    hi.bitcast(fp32), ALU.subtract)
                            nc.vector.tensor_tensor(dst2, ps[64:P, 2 * P:3 * P], hi2.bitcast(fp32),
                                                    ALU.subtract).then_inc(sem_, 1)

                        def x_lo(t):
                            dve.wait_ge(s_xhi, at(a, NT, t + 1))
                            cols = slice(t * P, (t + 1) * P)
                            low(xT[1][:, :, cols], xT2[64:P, cols], (ps_a, ps_b)[t], xT[0][:, :, cols], xT2[0:64, cols],
                                s_xlo, 0)

                        def q_lo(m):
                            dve.wait_ge(s_qhi, at(a, 3, m + 1))
                            ps = (ps_b, ps_b, ps_a)[m]
                            q = par(a)
                            if m < 2:
                                nc.vector.tensor_tensor(qT[q][1][:, m, :], ps[:, 0:S], qT[q][0][:, m, :].bitcast(fp32),
                                                        ALU.subtract).then_inc(s_qlo, 1)
                            else:
                                nc.vector.tensor_tensor(qT2[q][64:P, :], ps[64:P, 0:S], qT2[q][0:64, :].bitcast(fp32),
                                                        ALU.subtract).then_inc(s_qlo, 1)

                        def maxima(m):
                            h4, t = m // NT, m % NT
                            dve.wait_ge(s_mps, at(a, NT * QUADS, m + 1))
                            if m == 0:
                                dve.wait_ge(s_mk, at(a, 1, 1))
                            ps = ps_m[m % 2][:, 0:QUAD].rearrange("p (h k) -> p h k", k=KEYS)
                            nc.vector.tensor_tensor(ip_masked[m % 2][:], ps[:, :, T:KEYS],
                                                    stats[:, t:t + 1, R_MASK:R_MASK + NIP].broadcast_to([P, 4, NIP]),
                                                    ALU.add).then_inc(s_dve, 1)
                            nc.vector.tensor_reduce(stats[:, t, R_MT + 4 * h4:R_MT + 4 * h4 + 4], ps[:, :, 0:T], AX.X, ALU.max)
                            dve.wait_ge(s_dve, at(a, NT * QUADS, m + 1))
                            nc.vector.tensor_reduce(stats[:, t, R_MI + 4 * h4:R_MI + 4 * h4 + 4], ip_masked[m % 2][:],
                                                    AX.X, ALU.max).then_inc(s_mx, 1)

                        def invert(u):
                            dve.wait_ge(s_pv, at(c, UNITS, u + 1))
                            ns = 2 * GROUPS[u % 3]
                            o = ps_o[:, 0:ns * 17].rearrange("p (n c) -> p n c", c=17)
                            nc.vector.reciprocal(inv[:, 0:ns], o[:, :, 0]).then_inc(s_inv, 1)

                        def norm(u):
                            ns = 2 * GROUPS[u % 3]
                            o = ps_o[:, 0:ns * 17].rearrange("p (n c) -> p n c", c=17)
                            wait(dve, s_at, c, UNITS, u - 1)
                            dve.wait_ge(s_inv, at(c, UNITS, u + 1))
                            nc.vector.tensor_tensor(heads[u % 2][:, 0:ns, :], o[:, :, 1:17],
                                                    inv[:, 0:ns].rearrange("p (n o) -> p n o", o=1).broadcast_to([P, ns, DH]),
                                                    ALU.mult).then_inc(s_nm, 1)

                        def a_lo(c, t):
                            dve.wait_ge(s_ahi, at(c, NT, t + 1))
                            cols = slice(t * P, (t + 1) * P)
                            low(aT[1][:, :, cols], aT2[64:P, cols], (ps_b, ps_a)[t], aT[0][:, :, cols], aT2[0:64, cols], s_alo, 0)

                        def finish(c, t):
                            dve.wait_ge(s_op, at(c, NT, t + 1))
                            if t == 0:
                                dve.wait_ge(s_xk, at(c, NT, NT))
                                reg = c[0] is not None
                                if reg or c[1] >= 2:
                                    dve.wait_ge(s_y[par(c)], nth(c, 32, -32))
                            nc.vector.tensor_tensor(y[par(c)][:, t, :], ps_a[:, 0:D], x_keep[par(c)][:, t, :],
                                                    ALU.add).then_inc(s_yr, 1)

                        def spread_values(g):
                            if g == 0:
                                dve.wait_ge(s_vals[par(b)], nth(b, 16 * NVDMA))
                                wait(dve, s_pv, b, UNITS, -UNITS)
                            v = values[par(b)][:].rearrange("p (t n c) -> p t n c", t=TILES, c=SLOT)
                            t = slice(GTILE[g], GTILE[g] + GTILES[g])
                            nc.vector.tensor_tensor(
                                v[:, t, :, 2:SLOT],
                                raw_v[par(b)][:].rearrange("p t (o c) -> p t o c", o=1)[:, t]
                                .broadcast_to([P, GTILES[g], SLOTS, 3 * DH]),
                                own_rows[:].rearrange("p t (n c) -> p t n c", n=SLOTS)[:, t], ALU.mult).then_inc(s_vx, 1)

                        if A:
                            wait(dve, s_et, a, 1, 0)
                            nc.vector.tensor_copy(stats[:, :, R_MASK:R_MASK + NIP],
                                                  mask[:, :, bass.ds(at(a, NIP, 0), NIP)]).then_inc(s_mk, 1)
                        d = off(b, -2)
                        for s in range(PAIRS):
                            if A and s == 0:
                                x_lo(0)
                                x_lo(1)
                            if Ds and s == 1:
                                a_lo(d, 1)
                            if Ds and s == 2:
                                finish(d, 1)
                            if A and MAXIMA[s]:
                                maxima(MAXIMA[s][0])
                            if A and s in (1, 2, 3):
                                q_lo(s - 1)
                            if Cs and s == 4:
                                a_lo(c, 0)
                            if Cs and s == 5:
                                finish(c, 0)
                            if Cs and s < UNITS:
                                invert(s)
                            if A:
                                if s == 0:
                                    dve.wait_ge(s_keys[par(a)], nth(a, 16))
                                    wait(dve, s_sc, b, PAIRS, 0)
                                if s < 2:
                                    for g in ([0], [1, 2])[s]:
                                        spread_keys(nc.vector, a, 0, g)
                                for m in MAXIMA[s][1:2]:
                                    maxima(m)
                            if Cs and s < UNITS:
                                norm(s)
                            if A:
                                for m in MAXIMA[s][2:]:
                                    maxima(m)
                            if Bs and s in (4, 5, 6):
                                spread_values(s - 4)

                    sched(dve, step)

                @block.gpsimd
                def _(pool):
                    def step(pool, b, n):
                        A, Bs, Cs, Ds = has(n)
                        a, c = off(b, 1), off(b, -1)
                        for s in range(PAIRS):
                            if Bs:
                                pool.wait_ge(s_hi, at(b, PAIRS, s + 1))
                                w = S * (2 if 2 * s + 1 < TILES else 1)
                                nc.gpsimd.tensor_tensor(prob_lo[par(b)][:, s, 0:w], prob[:, s, 0:w],
                                                        prob_hi[par(b)][:, s, 0:w], ALU.subtract).then_inc(s_lo, 1)
                            if Cs and s < UNITS:
                                t, g = s // 3, s % 3
                                nh = GROUPS[g]
                                pool.wait_ge(s_nm, at(c, UNITS, s + 1))
                                wait(pool, s_att, c, NT, t + 1 - NT)
                                hv = heads[s % 2][:, 0:2 * nh, :].rearrange("p (h i) c -> p h i c", i=2)
                                for c0 in (GHEAD[g] * DH, D)[0:1 + g // 2]:
                                    last = nc.gpsimd.tensor_tensor(
                                        attn[:, t, c0:c0 + nh * DH].rearrange("p (h c) -> p h c", c=DH),
                                        hv[:, :, 0, :], hv[:, :, 1, :], ALU.add)
                                last.then_inc(s_at, 1)
                            if A and s in (0, 2, 4):
                                if s == 0:
                                    pool.wait_ge(s_keys[par(a)], nth(a, 16))
                                    wait(pool, s_sc, b, PAIRS, 0)
                                spread_keys(nc.gpsimd, a, 1, s // 2)

                    sched(pool, step)


_INS = ["x", "ctx_2048", "fside_Bx4x4_0", "L0_xattn_w_q", "L0_xattn_w_k", "L0_xattn_w_v", "L0_xattn_w_k_ip",
        "L0_xattn_w_v_ip", "L0_xattn_w_out", "L0_xattn_b_out"]


def kernel(**inputs):
    import concourse.bacc as _bacc
    from concourse.bass_utils import run_bass_kernel_spmd as _run

    nc = _bacc.Bacc("TRN2", target_bir_lowering=False, num_devices=1)
    arrays, args = {}, []
    named = [(n, np.ascontiguousarray(inputs[n])) for n in _INS] + list(constants().items())
    for name, a in named:
        arrays[f"in_{name}_dram"] = a
        args.append(nc.dram_tensor(f"in_{name}_dram", a.shape, mybir.dt.from_np(a.dtype), kind="ExternalInput").ap())
    shape = tuple(inputs["x"].shape)
    args.append(nc.dram_tensor("out_0_dram", shape, fp32, kind="ExternalOutput").ap())
    xattn_kernel(nc, *args, shape[0])
    r = _run(nc, [arrays], core_ids=[0])
    return r.results[0]["out_0_dram"]
```
